# Optimizing a Trainium2 kernel written in Bass

```python
import numpy as np
import jax
import jax.numpy as jnp

def _softmax(x, axis=-1):
    return jax.nn.softmax(x, axis=axis)

def _gelu(x):
    return jax.nn.gelu(x, approximate=True)

def _silu(x):
    return jax.nn.silu(x)

def _sigmoid(x):
    return jax.nn.sigmoid(x)

def _layernorm(x, axis=-1, eps=1e-05):
    m = jnp.mean(x, axis=axis, keepdims=True)
    v = jnp.var(x, axis=axis, keepdims=True)
    return (x - m) / jnp.sqrt(v + eps)

def _scatter_add(tgt, idx, src, axis=0):
    return tgt.at[idx].add(src)

def _segment_sum(src, seg, n):
    return jax.ops.segment_sum(src, seg, n)
kernel_name = 'mk_gnn_resnorm_d2_gnn_r16_f9fbe6'

def setup_inputs(seed: int=0):
    np.random.seed(seed)
    _w = jnp.asarray

    def _rec_inputs():
        import jax
        import jax.numpy as jnp
        _gk = jax.random.key(seed)
        x = -0.0002117 + 1 * jax.random.normal(jax.random.fold_in(_gk, 1), (6250, 256), jnp.float32)
        src = jax.random.randint(jax.random.fold_in(_gk, 2), (100000,), 0, 6250, jnp.int32)
        dst = jnp.minimum((6250 * jax.random.uniform(jax.random.fold_in(_gk, 3), (100000,)) ** 2.0).astype(jnp.int32), 99999)
        _o = jnp.argsort(dst, stable=True)
        src = src[_o]
        dst = dst[_o]
        edge_attr_194 = 0.000189139 + 1.00015 * jax.random.normal(jax.random.fold_in(_gk, 12), (100000, 194), jnp.float32)
        edge_weight = jax.random.uniform(jax.random.fold_in(_gk, 14), (100000,), jnp.float32, 0.0, 0.03125)
        return (x, src, dst, edge_attr_194, edge_weight)
    x, src, dst, edge_attr_194, edge_weight = _rec_inputs()

    def _L0_gnn_setup():
        import jax, jax.numpy as jnp
        import numpy as np
        N_NODES = 6250
        N_EDGES = 200000
        DIM = 256
        LEAKY_SLOPE = 0.2
        EPS = 1e-12
        key = jax.random.key(seed)
        ks = jax.random.split(key, 8)
        embeddings = jax.random.normal(ks[0], (N_NODES, DIM), dtype=jnp.float32)
        edge_src = jax.random.randint(ks[1], (N_EDGES,), 0, N_NODES, dtype=jnp.int32)
        edge_dst = jax.random.randint(ks[2], (N_EDGES,), 0, N_NODES, dtype=jnp.int32)
        edge_val = jax.random.uniform(ks[3], (N_EDGES,), dtype=jnp.float32) / 32.0
        scale = 1.0 / np.sqrt(DIM)
        W1 = jax.random.normal(ks[4], (DIM, DIM), dtype=jnp.float32) * scale
        b1 = jax.random.normal(ks[5], (DIM,), dtype=jnp.float32) * 0.01
        W2 = jax.random.normal(ks[6], (DIM, DIM), dtype=jnp.float32) * scale
        b2 = jax.random.normal(ks[7], (DIM,), dtype=jnp.float32) * 0.01
        return {'embeddings': embeddings, 'edge_src': edge_src, 'edge_dst': edge_dst, 'edge_val': edge_val, 'W1': W1, 'b1': b1, 'W2': W2, 'b2': b2}
    _L0_gnn_all = _L0_gnn_setup()
    _L0_gnn_in = {k: v for k, v in _L0_gnn_all.items() if k in ('W1', 'b1', 'W2', 'b2')}
    del _L0_gnn_all

    def _L1_gnn_setup():
        import jax, jax.numpy as jnp
        import numpy as np
        N = 3125
        E = 15625
        IN = 256
        OUT = 256
        H = 4
        C = OUT // H
        MSG = 128
        TIME = 64
        ED = MSG + TIME + 2

        def _glorot(k, shape):
            return (jax.random.normal(k, shape, jnp.float32) / np.sqrt(shape[0])).astype(jnp.float32)

        def _tconv(x, src, dst, edge_attr, Wq, bq, Wk, bk, Wv, bv, We, Ws, bs):
            n = x.shape[0]
            q = (x @ Wq + bq).reshape(n, H, C)
            k = (x @ Wk + bk).reshape(n, H, C)
            v = (x @ Wv + bv).reshape(n, H, C)
            e = (edge_attr @ We).reshape(-1, H, C)
            kj = k[src] + e
            vj = v[src] + e
            logits = jnp.einsum('ehc,ehc->eh', q[dst], kj) / np.sqrt(C)
            m = jax.lax.stop_gradient(jax.ops.segment_max(logits, dst, num_segments=n))
            ex = jnp.exp(logits - m[dst])
            denom = jax.ops.segment_sum(ex, dst, num_segments=n)
            a = ex / (denom[dst] + 1e-16)
            agg = jax.ops.segment_sum(vj * a[:, :, None], dst, num_segments=n)
            return agg.reshape(n, H * C) + x @ Ws + bs
        ks = jax.random.split(jax.random.key(seed), 16)
        z = lambda: jnp.zeros((H * C,), jnp.float32)
        inp = {'x': jax.random.normal(ks[0], (N, IN), jnp.float32), 'edge_index': jax.random.randint(ks[1], (2, E), 0, N), 'edge_attr': jax.random.normal(ks[2], (E, ED), jnp.float32), 'Wq1': _glorot(ks[3], (IN, H * C)), 'bq1': z(), 'Wk1': _glorot(ks[4], (IN, H * C)), 'bk1': z(), 'Wv1': _glorot(ks[5], (IN, H * C)), 'bv1': z(), 'We1': _glorot(ks[6], (ED, H * C)), 'Ws1': _glorot(ks[7], (IN, H * C)), 'bs1': z(), 'Wq2': _glorot(ks[8], (OUT, H * C)), 'bq2': z(), 'Wk2': _glorot(ks[9], (OUT, H * C)), 'bk2': z(), 'Wv2': _glorot(ks[10], (OUT, H * C)), 'bv2': z(), 'We2': _glorot(ks[11], (ED, H * C)), 'Ws2': _glorot(ks[12], (OUT, H * C)), 'bs2': z()}
        return inp
    _L1_gnn_all = _L1_gnn_setup()
    _L1_gnn_in = {k: v for k, v in _L1_gnn_all.items() if k in ('Wq1', 'bq1', 'Wk1', 'bk1', 'Wv1', 'bv1', 'We1', 'Ws1', 'bs1', 'Wq2', 'bq2', 'Wk2', 'bk2', 'Wv2', 'bv2', 'We2', 'Ws2', 'bs2')}
    del _L1_gnn_all
    return {'x': x, 'src': src, 'dst': dst, 'edge_attr_194': edge_attr_194, 'edge_weight': edge_weight, 'L0_gnn_W1': _L0_gnn_in['W1'], 'L0_gnn_b1': _L0_gnn_in['b1'], 'L0_gnn_W2': _L0_gnn_in['W2'], 'L0_gnn_b2': _L0_gnn_in['b2'], 'L1_gnn_Wq1': _L1_gnn_in['Wq1'], 'L1_gnn_bq1': _L1_gnn_in['bq1'], 'L1_gnn_Wk1': _L1_gnn_in['Wk1'], 'L1_gnn_bk1': _L1_gnn_in['bk1'], 'L1_gnn_Wv1': _L1_gnn_in['Wv1'], 'L1_gnn_bv1': _L1_gnn_in['bv1'], 'L1_gnn_We1': _L1_gnn_in['We1'], 'L1_gnn_Ws1': _L1_gnn_in['Ws1'], 'L1_gnn_bs1': _L1_gnn_in['bs1'], 'L1_gnn_Wq2': _L1_gnn_in['Wq2'], 'L1_gnn_bq2': _L1_gnn_in['bq2'], 'L1_gnn_Wk2': _L1_gnn_in['Wk2'], 'L1_gnn_bk2': _L1_gnn_in['bk2'], 'L1_gnn_Wv2': _L1_gnn_in['Wv2'], 'L1_gnn_bv2': _L1_gnn_in['bv2'], 'L1_gnn_We2': _L1_gnn_in['We2'], 'L1_gnn_Ws2': _L1_gnn_in['Ws2'], 'L1_gnn_bs2': _L1_gnn_in['bs2']}

def reference(x, src, dst, edge_attr_194, edge_weight, L0_gnn_W1, L0_gnn_b1, L0_gnn_W2, L0_gnn_b2, L1_gnn_Wq1, L1_gnn_bq1, L1_gnn_Wk1, L1_gnn_bk1, L1_gnn_Wv1, L1_gnn_bv1, L1_gnn_We1, L1_gnn_Ws1, L1_gnn_bs1, L1_gnn_Wq2, L1_gnn_bq2, L1_gnn_Wk2, L1_gnn_bk2, L1_gnn_Wv2, L1_gnn_bv2, L1_gnn_We2, L1_gnn_Ws2, L1_gnn_bs2):
    import jax
    import jax.numpy as jnp

    def _L0_gnn_ref(embeddings, edge_src, edge_dst, edge_val, W1, b1, W2, b2):
        import jax, jax.numpy as jnp
        import numpy as np
        N_NODES = 6250
        N_EDGES = 200000
        DIM = 256
        LEAKY_SLOPE = 0.2
        EPS = 1e-12
        ego_emb = embeddings @ W1.T + b1
        messages = edge_val[:, None] * embeddings[edge_src]
        neighbor_emb = jax.ops.segment_sum(messages, edge_dst, num_segments=embeddings.shape[0])
        interaction_emb = neighbor_emb * embeddings
        side_emb = (neighbor_emb + interaction_emb) @ W2.T + b2
        out = ego_emb + side_emb
        out = jnp.where(out >= 0, out, LEAKY_SLOPE * out)
        norm = jnp.sqrt(jnp.sum(out * out, axis=1, keepdims=True))
        return out / jnp.maximum(norm, EPS)

    def _L1_gnn_ref(x, edge_index, edge_attr, Wq1, bq1, Wk1, bk1, Wv1, bv1, We1, Ws1, bs1, Wq2, bq2, Wk2, bk2, Wv2, bv2, We2, Ws2, bs2):
        import jax, jax.numpy as jnp
        import numpy as np
        N = 3125
        E = 15625
        IN = 256
        OUT = 256
        H = 4
        C = OUT // H
        MSG = 128
        TIME = 64
        ED = MSG + TIME + 2

        def _glorot(k, shape):
            return (jax.random.normal(k, shape, jnp.float32) / np.sqrt(shape[0])).astype(jnp.float32)

        def _tconv(x, src, dst, edge_attr, Wq, bq, Wk, bk, Wv, bv, We, Ws, bs):
            n = x.shape[0]
            q = (x @ Wq + bq).reshape(n, H, C)
            k = (x @ Wk + bk).reshape(n, H, C)
            v = (x @ Wv + bv).reshape(n, H, C)
            e = (edge_attr @ We).reshape(-1, H, C)
            kj = k[src] + e
            vj = v[src] + e
            logits = jnp.einsum('ehc,ehc->eh', q[dst], kj) / np.sqrt(C)
            m = jax.lax.stop_gradient(jax.ops.segment_max(logits, dst, num_segments=n))
            ex = jnp.exp(logits - m[dst])
            denom = jax.ops.segment_sum(ex, dst, num_segments=n)
            a = ex / (denom[dst] + 1e-16)
            agg = jax.ops.segment_sum(vj * a[:, :, None], dst, num_segments=n)
            return agg.reshape(n, H * C) + x @ Ws + bs
        src, dst = (edge_index[0], edge_index[1])
        h = jax.nn.relu(_tconv(x, src, dst, edge_attr, Wq1, bq1, Wk1, bk1, Wv1, bv1, We1, Ws1, bs1))
        return _tconv(h, src, dst, edge_attr, Wq2, bq2, Wk2, bk2, Wv2, bv2, We2, Ws2, bs2)
    edge_index = jnp.stack([src, dst])
    x = _layernorm(x + _L0_gnn_ref(x, src, dst, edge_weight, L0_gnn_W1, L0_gnn_b1, L0_gnn_W2, L0_gnn_b2), axis=-1)
    x = _layernorm(x + _L1_gnn_ref(x, edge_index, edge_attr_194, L1_gnn_Wq1, L1_gnn_bq1, L1_gnn_Wk1, L1_gnn_bk1, L1_gnn_Wv1, L1_gnn_bv1, L1_gnn_We1, L1_gnn_Ws1, L1_gnn_bs1, L1_gnn_Wq2, L1_gnn_bq2, L1_gnn_Wk2, L1_gnn_bk2, L1_gnn_Wv2, L1_gnn_bv2, L1_gnn_We2, L1_gnn_Ws2, L1_gnn_bs2), axis=-1)
    return x

_drawn_inputs = setup_inputs


def setup_inputs(seed=0):
    import zlib

    import numpy as np

    out = dict(_drawn_inputs(seed))
    spreads = {'L1_gnn_bq1': (0.0, 0.1),
     'L1_gnn_bk1': (0.0, 2.0),
     'L1_gnn_bv1': (0.0, 0.1),
     'L1_gnn_bs1': (0.0, 0.1),
     'L1_gnn_bq2': (0.0, 0.1),
     'L1_gnn_bk2': (0.0, 2.0),
     'L1_gnn_bv2': (0.0, 0.1),
     'L1_gnn_bs2': (0.0, 0.1)}
    factors = {'edge_weight': 8.0,
     'L0_gnn_b1': 64.0,
     'L0_gnn_W2': 8.0,
     'L0_gnn_b2': 64.0,
     'L0_gnn_W1': 4.484}
    for name, (base, spread) in spreads.items():
        noise = np.random.default_rng([zlib.crc32(name.encode()), seed]).standard_normal(out[name].shape)
        drawn = base * np.exp(spread * noise) if base else spread * noise
        out[name] = jnp.asarray(drawn.astype(out[name].dtype))
    for name, factor in factors.items():
        out[name] = (out[name] * factor).astype(out[name].dtype)
    return out
```

```python
from contextlib import ExitStack

import numpy as np

import concourse.bass as bass
from concourse import mybir

P = 128
OWN = P - 1
D = 256
H = 4
C = D // H
KD = D // P
BATCH = 31
ROWS = 32
VALS = D + H
BIG = float(2.0 ** 100)
LEAKY = 0.2
NORM_EPS = 1e-12
LN_EPS = 1e-5
SUM_EPS = 1e-16

F32 = mybir.dt.float32
BF16 = mybir.dt.bfloat16
I32 = mybir.dt.int32
ALU = mybir.AluOpType
ACT = mybir.ActivationFunctionType


class Shapes:
    def __init__(self, nodes, edges, attrs):
        self.nodes, self.edges, self.attrs = nodes, edges, attrs
        self.tiles = -(-edges // OWN)
        self.blocks = -(-nodes // P)
        self.rows = self.blocks * P
        self.cols = self.tiles * OWN + 1
        self.ka = -(-attrs // 32) * 16
        self.front, self.behind = self.rows - 2, self.rows - 1
        assert nodes <= self.rows - 2


class Lane:

    def __init__(self, sem):
        self.sem, self.count, self.program, self.seen = sem, 0, [], {}

    def _add(self, build, after, sem, step):
        waits = []
        for mark in after:
            if mark is not None and self.seen.get(id(mark[0]), 0) < mark[1]:
                self.seen[id(mark[0])] = mark[1]
                waits.append(mark)
        self.program.append((waits, build, sem, step))

    def do(self, build, after=()):
        self._add(build, after, self.sem, 1)
        self.count += 1
        return self.sem, self.count

    def dma(self, build, slot, after=()):
        self._add(build, after, slot.sem, 16)
        slot.count += 16
        return slot.sem, slot.count

    def hold(self, after):
        self._add(None, after, None, 0)

    def play(self, eng):
        for waits, build, sem, step in self.program:
            for s, value in waits:
                eng.wait_ge(s, value)
            if build is not None:
                build(eng).then_inc(sem, step)


class Slot:
    def __init__(self, sem):
        self.sem, self.count = sem, 0


class Phase:

    def __init__(self, nc, name):
        self.nc, self.name, self.stack = nc, name, ExitStack()

    def __enter__(self):
        self.stack.__enter__()
        self.pe, self.dve, self.act, self.pool, self.sp = (
            Lane(self.sem(n)) for n in ("pe", "dve", "act", "pool", "sp"))
        return self

    def sb(self, name, shape, dtype=F32):
        return self.stack.enter_context(self.nc.sbuf_tensor(f"{self.name}_{name}", shape, dtype))

    def psum(self, name):
        return self.stack.enter_context(self.nc.psum_tensor(f"{self.name}_{name}", [P, 512], F32))

    def sem(self, name):
        return self.stack.enter_context(self.nc.semaphore(f"{self.name}_{name}_done"))

    def slots(self, name, n):
        return [Slot(self.sem(f"{name}{i}")) for i in range(n)]

    def __exit__(self, kind, *rest):
        if kind is None:
            with self.nc.Block() as block:
                for start, lane in ((block.tensor, self.pe), (block.vector, self.dve), (block.scalar, self.act),
                                    (block.gpsimd, self.pool), (block.sync, self.sp)):
                    start(lane.play)
        return self.stack.__exit__(kind, *rest)


def rows_of(table, index):
    return dict(in_=table, in_offset=bass.IndirectOffsetOnAxis(ap=index, axis=0))



def constants(nc, keep, t, s):
    k = {}

    def sb(name, shape, dtype=F32):
        k[name] = keep.enter_context(nc.sbuf_tensor(name, shape, dtype))
        return k[name]

    ident = sb("ident", [P, P])
    slot_of = sb("slot_of", [P, P])
    upto = sb("upto", [P, P])
    run_end = sb("run_end", [P, s.tiles])
    src = sb("src_sb", [P, s.tiles], I32)
    dst = sb("dst_sb", [P, s.tiles], I32)
    weight = sb("weight_sb", [P, s.tiles])
    last_row = sb("last_row", [P, s.blocks], I32)
    has_edge = sb("has_edge", [P, s.blocks])

    groups = -(-s.tiles // P)
    with Phase(nc, "setup") as ph:
        pe, dve, pool, sp = ph.pe, ph.dve, ph.pool, ph.sp
        load = ph.slots("load", 5)
        got_src = sp.dma(lambda e: e.dma_start(src[:], t["src_cols"]), load[0])
        got_dst = sp.dma(lambda e: e.dma_start(dst[:], t["dst_cols"]), load[0])
        got_w = sp.dma(lambda e: e.dma_start(weight[:], t["weight_cols"]), load[0])

        z = pool.do(lambda e: e.memset(ident[:], 0.0))
        m_id = pool.do(lambda e: e.affine_select(
            out=ident[:], in_=ident[:], compare_op=ALU.not_equal, fill=1.0, base=0,
            pattern=[[-1, P]], channel_multiplier=1), [z])
        iota = ph.sb("iota", [P, P])
        m_io = pool.do(lambda e: e.iota(iota[:], pattern=[[1, P]], base=0, channel_multiplier=0,
                                        allow_small_or_imprecise_dtypes=True))
        a = pool.do(lambda e: e.iota(slot_of[:], pattern=[[1, P]], base=0, channel_multiplier=0,
                                     allow_small_or_imprecise_dtypes=True))
        a = pool.do(lambda e: e.memset(slot_of[:, 0:1], float(P - 1)), [a])
        b = pool.do(lambda e: e.memset(upto[:], 1.0))
        b = pool.do(lambda e: e.affine_select(
            out=upto[:], in_=upto[:], compare_op=ALU.is_ge, fill=0.0, base=0,
            pattern=[[1, P]], channel_multiplier=-1), [b])
        b = pool.do(lambda e: e.memset(upto[:, 0:1], 1.0), [b])

        d_int = [ph.sb(f"d_int{i}", [P, P], I32) for i in range(2)]
        d_f = [ph.sb(f"d_f{i}", [P, P]) for i in range(2)]
        same = [ph.sb(f"same{i}", [P, P]) for i in range(2)]
        ends = [ph.sb(f"ends{i}", [P, P]) for i in range(2)]
        turned = ph.psum("turned")
        zero = [dve.do(lambda e, x=x: e.memset(x[:], 0.0)) for x in same + ends]
        same_m = zero[:2]
        copied = [None, None]
        pe_read = [zero[2], zero[3]]
        for g in range(groups):
            n, u = min(P, s.tiles - g * P), g % 2
            m = sp.dma(lambda e, g=g, n=n, u=u: e.dma_start(d_int[u][0:n, :], t["dst_rows"][g * P:g * P + n, :]),
                       load[1 + u], [copied[u]])
            m = copied[u] = dve.do(lambda e, n=n, u=u: e.tensor_copy(d_f[u][0:n, :], d_int[u][0:n, :]), [m, same_m[u]])
            m = same_m[u] = dve.do(lambda e, n=n, u=u: e.tensor_tensor(
                same[u][0:n, 0:P - 1], d_f[u][0:n, 1:P], d_f[u][0:n, 0:P - 1], ALU.is_equal), [m, same_m[u]])
            m = dve.do(lambda e, n=n, u=u: e.tensor_tensor_scan(
                ends[u][0:n, ::-1], same[u][0:n, ::-1], iota[0:n, ::-1], 0.0, ALU.mult, ALU.max),
                [m, m_io, pe_read[u]])
            m = pe_read[u] = pe.do(lambda e, n=n, u=u: e.transpose(
                turned[:, u * P:u * P + n], ends[u][0:n, :], ident[0:n, 0:n]), [m, m_id])
            dve.do(lambda e, g=g, n=n, u=u: e.tensor_copy(
                run_end[:, g * P:g * P + n], turned[:, u * P:u * P + n]), [m])
            pe_read[u] = (dve.sem, dve.count)
        sp.hold([got_src, got_dst, got_w])
    return k


def single_rows(nc, keep, t, s):
    batches = -(-s.tiles // BATCH)
    singles = keep.enter_context(nc.sbuf_tensor("singles", [1, batches, H * ROWS + 1], F32))
    with Phase(nc, "single") as ph:
        dve, sp = ph.dve, ph.sp
        ends = ph.sb("ends", [1, 2, s.tiles], I32)
        endf = ph.sb("endf", [1, 2, s.tiles])
        pen = ph.sb("pen", [1, s.tiles])
        load = ph.slots("load", 1)[0]
        sp.dma(lambda e: e.dma_start(ends[:, 0, :], t["dst_cols"][0:1, :]), load)
        m = sp.dma(lambda e: e.dma_start(ends[:, 1, :], t["dst_cols"][P - 1:P, :]), load)
        z = dve.do(lambda e: e.memset(singles[:], -BIG))
        m = dve.do(lambda e: e.tensor_copy(endf[:], ends[:]), [m])
        m = dve.do(lambda e: e.tensor_tensor(pen[:], endf[:, 0, :], endf[:, 1, :], ALU.not_equal), [m])
        m = dve.do(lambda e: e.tensor_scalar(pen[:], pen[:], -BIG, None, ALU.mult), [m])
        for j in range(batches):
            n = min(BATCH, s.tiles - j * BATCH)
            for h in range(H):
                dve.do(lambda e, j=j, n=n, h=h: e.tensor_copy(
                    singles[:, j, ROWS * h + 1:ROWS * h + 1 + n], pen[:, j * BATCH:j * BATCH + n]), [m, z])
    return singles



class RunSums:

    GROUP = 4
    RING = 4

    def __init__(self, ph, k, s, width, table):
        self.ph, self.k, self.s, self.width, self.table = ph, k, s, width, table
        self.mask = ph.sb("run_mask", [P, self.RING, P])
        self.vals = ph.sb("vals", [P, self.RING, width])
        self.out = [ph.psum("sum0"), ph.psum("sum1")]
        self.rows = ph.sb("sum_rows", [P, 2, self.GROUP, width])
        self.stores = ph.slots("store", 2)
        self.product, self.evac, self.stored = {}, {}, {}
        self.view = table.rearrange("(t p) c -> p t c", p=P)

    def make_mask(self, i):
        k, u = self.k, i % self.RING
        return self.ph.dve.do(lambda e: e.scalar_tensor_tensor(
            self.mask[:, u, :], k["slot_of"][:], k["run_end"][:, i:i + 1], k["upto"][:], ALU.is_le, ALU.mult),
            [self.product.get(i - self.RING)])

    def carry(self, i, after, scale=None):
        act, dve, v = self.ph.act, self.ph.dve, self.vals
        w, u = self.width, i % self.RING
        if i == 0:
            return dve.do(lambda e: e.memset(v[0:1, u, :], 0.0), after)
        prev = self.out[(i - 1) % 2]
        m = act.do(lambda e: e.activation(v[0:1, u, :], prev[0:1, 0:w], ACT.Copy), after + [self.product[i - 1]])
        if scale is None:
            return m
        row = v[0:1, u, 0:D].rearrange("p (h c) -> p h c", h=H)
        m = dve.do(lambda e: e.tensor_tensor(row, row, scale.unsqueeze(2).to_broadcast([1, H, C]), ALU.mult), [m])
        return dve.do(lambda e: e.tensor_tensor(v[0:1, u, D:w], v[0:1, u, D:w], scale, ALU.mult), [m])

    def sum(self, i, after):
        ph, w, u = self.ph, self.width, i % self.RING
        out = self.out[i % 2]
        self.product[i] = ph.pe.do(lambda e: e.matmul(
            out[:, 0:w], self.mask[:, u, :], self.vals[:, u, :], start=True, stop=True),
            after + [self.evac.get(i - 2)])

    def keep(self, i):
        ph, w, grp, out = self.ph, self.width, self.GROUP, self.out[i % 2]
        g, q = i // grp, i % grp
        self.evac[i] = ph.act.do(lambda e: e.activation(
            self.rows[:, g % 2, q, :], out[:, 0:w], ACT.Copy), [self.product[i], self.stored.get(g - 2)])
        if q == grp - 1 or i == self.s.tiles - 1:
            self.stored[g] = ph.sp.dma(lambda e: e.dma_start(
                self.view[:, g * grp:g * grp + q + 1, :], self.rows[:, g % 2, 0:q + 1, :]),
                self.stores[g % 2], [self.evac[i]])

    def finish(self):
        self.ph.sp.hold([(x.sem, x.count) for x in self.stores])


def edge_pass_weighted(nc, k, t, s, table):
    with Phase(nc, "e0") as ph:
        pe, dve, act, pool, sp = ph.pe, ph.dve, ph.act, ph.pool, ph.sp
        NX = 6
        x = ph.sb("x", [P, NX, D])
        got = ph.slots("x", NX)
        sums = RunSums(ph, k, s, D, table)
        ident = k["ident"]

        load = ph.slots("load", 1)[0]
        num = ph.sb("num", [P, s.tiles], I32)
        part = ph.sb("part", [P, s.tiles], I32)
        hi = ph.sb("hi", [P, s.tiles])
        lo = ph.sb("lo", [P, s.tiles])
        iota = ph.sb("iota", [P, P], BF16)
        one_hi = ph.sb("one_hi", [P, 2, s.blocks], BF16)
        one_lo = ph.sb("one_lo", [P, 2, P], BF16)
        count = ph.psum("count")
        m = sp.dma(lambda e: e.dma_start(num[:], t["dst_next_cols"]), load)
        m1 = dve.do(lambda e: e.tensor_scalar(part[:], num[:], P.bit_length() - 1, None, ALU.arith_shift_right), [m])
        m_hi = dve.do(lambda e: e.tensor_copy(hi[:], part[:]), [m1])
        m2 = dve.do(lambda e: e.tensor_scalar(part[:], num[:], P - 1, None, ALU.bitwise_and), [m_hi])
        m_lo = dve.do(lambda e: e.tensor_copy(lo[:], part[:]), [m2])
        m_io = pool.do(lambda e: e.iota(iota[:], pattern=[[1, P]], base=0, channel_multiplier=0,
                                        allow_small_or_imprecise_dtypes=True))
        counted = {}
        weighted, carried = {}, {}
        mask = {}
        R = sums.RING
        for i in range(s.tiles + 2):
            if i < s.tiles:
                u = i % NX
                m_x = pool.dma(lambda e, i=i, u=u: e.indirect_dma_start(
                    out=x[:, u, :], out_offset=None, **rows_of(t["x_rows"], k["src_sb"][:, i:i + 1])),
                    got[u], [weighted.get(i - NX)])
                mask[i] = sums.make_mask(i)
                m = dve.do(lambda e, i=i: e.tensor_scalar(one_lo[:, i % 2, :], iota[:], lo[:, i:i + 1], None, ALU.is_equal),
                           [m_lo, m_io, counted.get(i - 2)])
                m = dve.do(lambda e, i=i: e.tensor_scalar(one_hi[:, i % 2, :], iota[:, 0:s.blocks], hi[:, i:i + 1], None,
                                                          ALU.is_equal), [m_hi, counted.get(i - 2)])
                counted[i] = pe.do(lambda e, i=i: e.matmul(
                    count[0:s.blocks, 0:P], one_hi[:, i % 2, :], one_lo[:, i % 2, :],
                    start=(i == 0), stop=(i == s.tiles - 1)), [m])
                weighted[i] = dve.do(lambda e, i=i, u=u: e.tensor_scalar(
                    sums.vals[:, i % R, :], x[:, u, :], k["weight_sb"][:, i:i + 1], None, ALU.mult),
                    [m_x, sums.product.get(i - R)])
            if 0 <= i - 1 < s.tiles:
                c = sums.carry(i - 1, [weighted[i - 1]])
                sums.sum(i - 1, [mask[i - 1], c])
            if 0 <= i - 2:
                sums.keep(i - 2)
        sums.finish()

        B = s.blocks
        cnt = ph.sb("cnt", [B, P])
        run = ph.sb("run", [B, P])
        before = ph.sb("before", [B, B])
        has = ph.sb("has", [B, P])
        base = ph.sb("base", [B, 1])
        small = ph.psum("small")
        m_b = pool.do(lambda e: e.memset(before[:], 1.0))
        m_b = pool.do(lambda e: e.affine_select(
            out=before[:], in_=before[:], compare_op=ALU.is_ge, fill=0.0, base=-1,
            pattern=[[1, B]], channel_multiplier=-1), [m_b])
        m = dve.do(lambda e: e.tensor_copy(cnt[:], count[0:B, 0:P]), [counted[s.tiles - 1]])
        m_has = dve.do(lambda e: e.tensor_scalar(has[:], cnt[:], 0.0, None, ALU.is_gt), [m])
        m = dve.do(lambda e: e.tensor_tensor_scan(run[:], cnt[:], cnt[:], 0.0, ALU.add, ALU.bypass), [m])
        m2 = pe.do(lambda e: e.matmul(small[0:B, 0:1], before[:], run[:, P - 1:P], start=True, stop=True), [m, m_b])
        m2 = dve.do(lambda e: e.tensor_copy(base[:], small[0:B, 0:1]), [m2])
        m = dve.do(lambda e: e.tensor_scalar(run[:], run[:], base[:, 0:1], -1.0, ALU.add, ALU.add), [m, m2])
        m = dve.do(lambda e: e.tensor_scalar(run[:], run[:], 0.0, None, ALU.max), [m])
        m = pe.do(lambda e: e.transpose(small[:, 128:128 + B], run[:], ident[0:B, 0:B]), [m, m2])
        m_has = pe.do(lambda e: e.transpose(small[:, 256:256 + B], has[:], ident[0:B, 0:B]), [m_has])
        dve.do(lambda e: e.tensor_copy(k["last_row"][:], small[:, 128:128 + B]), [m_has])
        dve.do(lambda e: e.tensor_copy(k["has_edge"][:], small[:, 256:256 + B]), [m_has])


def edge_pass_attention(nc, name, k, t, s, w_edge, kv_rows, q_rows, singles, table):
    CH = 8
    STEPS = 14
    LAG = BATCH + STEPS
    NV, NKV, NQ, NE = LAG + 4, 6, 6, 3
    ident = k["ident"]
    batches = -(-s.tiles // BATCH)
    T = s.tiles
    with Phase(nc, name) as ph:
        pe, dve, act, pool, sp = ph.pe, ph.dve, ph.act, ph.pool, ph.sp
        sums = RunSums(ph, k, s, VALS, table)
        we = ph.sb("we", [s.ka, 2, D])
        ea = ph.sb("ea", [s.ka, NE, 2, CH * OWN + 1])
        kv = ph.sb("kv", [P, NKV, 2, D])
        q = ph.sb("q", [P, NQ, D])
        kj = ph.sb("kj", [P, 2, D])
        vj = ph.sb("vj", [P, NV, D])
        logit = ph.sb("logit", [P, 2, H, ROWS])
        ex = ph.sb("ex", [P, 2, H, ROWS])
        pe_e = [ph.psum("e0"), ph.psum("e1")]
        flat, back, small = ph.psum("flat"), ph.psum("back"), ph.psum("small")
        d_int = ph.sb("d_int", [P, 2, P], I32)
        d_f = ph.sb("d_f", [P, P])
        pen = ph.sb("pen", [P, 2, P + 1])
        lr = ph.sb("lr", [P, 2, P])
        fw = ph.sb("fw", [P, P])
        mx = ph.sb("mx", [P, P])
        ends = ph.sb("ends", [P, 2])
        RW = H * ROWS
        row_f = ph.sb("row_f", [1, RW + 2])
        row_b = ph.sb("row_b", [1, RW + 2])
        out_f = ph.sb("out_f", [1, RW + 2])
        out_b = ph.sb("out_b", [1, RW + 2])
        old = ph.sb("old", [1, H])
        scale = ph.sb("scale", [1, 2, H])
        got_kv, got_q, got_ea, got_d = (ph.slots(n, c) for n, c in (("kv", NKV), ("q", NQ), ("ea", NE), ("d", 2)))
        w_slot = ph.slots("w", 1)[0]

        got_w = sp.dma(lambda e: e.dma_start(we[:], w_edge), w_slot)
        z0 = dve.do(lambda e: e.memset(logit[:], 0.0))
        z1 = dve.do(lambda e: e.memset(pen[:], 0.0))
        z2 = dve.do(lambda e: e.memset(row_f[:], -BIG))
        z3 = dve.do(lambda e: e.memset(out_f[:], -BIG))
        z4 = dve.do(lambda e: e.memset(out_b[:], -BIG))
        z5 = dve.do(lambda e: e.memset(old[:], -BIG))

        ea_mark, ea_read, e_done = {}, {}, {}
        kj_read, v_written, v_read, dots = {}, {}, {}, {}
        turned, ex_ready, scaled = {}, {}, {}
        st = {}
        pen_read, lr_read, ex_read = {}, {}, {}

        def load_attrs(c):
            n = min(CH, T - c * CH) * OWN + 1
            ea_mark[c] = sp.dma(lambda e: e.dma_start(
                ea[:, c % NE, :, 0:n], t["attr_cols"][:, :, c * CH * OWN:c * CH * OWN + n]),
                got_ea[c % NE], [ea_read.get(c - NE)])

        def gather(i):
            u, w = i % NKV, i % NQ
            st["kv", i] = pool.dma(lambda e: e.indirect_dma_start(
                out=kv[:, u, :, :].rearrange("p a d -> p (a d)"), out_offset=None,
                **rows_of(kv_rows, k["src_sb"][:, i:i + 1])), got_kv[u], [v_written.get(i - NKV), kj_read.get(i - NKV)])
            st["q", i] = pool.dma(lambda e: e.indirect_dma_start(
                out=q[:, w, :], out_offset=None, **rows_of(q_rows, k["dst_sb"][:, i:i + 1])),
                got_q[w], [dots.get(i - NQ)])

        edge_done = {}

        def edge_product(i):
            c, off = i // CH, (i % CH) * OWN
            for a in range(2):
                m = pe.do(lambda e, a=a: e.matmul(
                    pe_e[i % 2][:, 0:D], ea[:, c % NE, a, off:off + P], we[:, a, :], start=(a == 0), stop=(a == 1)),
                    [ea_mark[c], got_w, v_written.get(i - 2), kj_read.get(i - 2)])
            ea_read[c] = edge_done[i] = m

        def logits(i):
            m, j, r = edge_done[i], i // BATCH, i % BATCH + 1
            mk = kj_read[i] = dve.do(lambda e: e.tensor_tensor(
                kj[:, i % 2, :], kv[:, i % NKV, 0, :], pe_e[i % 2][:, 0:D], ALU.add), [st["kv", i], m, dots.get(i - 2)])
            v_written[i] = dve.do(lambda e: e.tensor_tensor(
                vj[:, i % NV, :], kv[:, i % NKV, 1, :], pe_e[i % 2][:, 0:D], ALU.add), [v_read.get(i - NV)])
            for h in range(H):
                hs = slice(h * C, h * C + C)
                m = dve.do(lambda e, h=h, hs=hs: e.tensor_tensor_reduce(
                    kj[:, i % 2, hs], kj[:, i % 2, hs], q[:, i % NQ, hs], 1.0, 0.0, ALU.mult, ALU.add,
                    logit[:, j % 2, h, r:r + 1]), [mk, st["q", i], z0, turned.get(j - 2)])
            dots[i] = m

        def penalties(j):
            n = min(BATCH, T - j * BATCH)
            for h in range(H):
                m = sp.dma(lambda e, h=h: e.dma_start(
                    d_int[ROWS * h + 1:ROWS * h + 1 + n, j % 2, :], t["dst_rows"][j * BATCH:j * BATCH + n, :]),
                    got_d[j % 2], [st.get(("d", j - 2)), st["dz"]])
            m = st["d", j] = dve.do(lambda e: e.tensor_copy(d_f[:], d_int[:, j % 2, :]), [m, st.get(("ne", j - 1))])
            m = st["ne", j] = dve.do(lambda e: e.tensor_tensor(
                pen[:, j % 2, 1:P], d_f[:, 1:P], d_f[:, 0:P - 1], ALU.not_equal), [m, z1, pen_read.get(j - 2)])
            st["pen", j] = dve.do(lambda e: e.tensor_scalar(
                pen[:, j % 2, 1:P], pen[:, j % 2, 1:P], -BIG, None, ALU.mult), [m])

        st["dz"] = dve.do(lambda e: e.memset(d_int[:], 0))

        def forward(out, data, j, initial, after):
            return dve.do(lambda e: e.tensor_tensor_scan(
                out[:], pen[:, j % 2, 0:P], data, initial, ALU.add, ALU.max), after)

        def backward(out, data, j, initial, after):
            return dve.do(lambda e: e.tensor_tensor_scan(
                out[:, ::-1], pen[:, j % 2, 1:P + 1][:, ::-1], data[:, ::-1], initial, ALU.add, ALU.max), after)

        def setup_step(j, step):
            n = min(BATCH, T - j * BATCH)
            last = j * BATCH + n - 1
            lrj = lr[:, j % 2, :]
            if step == 0:
                m = turned[j] = pe.do(lambda e: e.transpose(
                    flat[:, 0:P], logit[:, j % 2, :, :].rearrange("p h r -> p (h r)"), ident[:]),
                    [dots[last], st.get("lr")])
                st["lr"] = act.do(lambda e: e.activation(
                    lrj, flat[:, 0:P], ACT.Copy, scale=1.0 / float(np.sqrt(C))), [m, lr_read.get(j - 2)])
            elif step == 1:
                m = forward(fw, lrj, j, -BIG, [st["lr"], st["pen", j], st.get("mx")])
                st["mx0"] = backward(mx, fw[:], j, -BIG, [m, st.get("exd"), st.get("edge_rows")])
            elif step == 2:
                m = pe.do(lambda e: e.transpose(small[0:1, 0:RW], mx[:, P - 1:P], ident[:]), [st["mx0"], st.get("small")])
                st["firsts"] = pe.do(lambda e: e.transpose(small[0:1, RW:2 * RW], mx[:, 0:1], ident[:]), [m])
            elif step == 3:
                both = []
                z = [z2, dve.do(lambda e: e.memset(row_b[:], -BIG), [st.get("outs")])]
                for row, at in ((row_f, 0), (row_b, RW)):
                    both.append(dve.do(lambda e, row=row, at=at: e.tensor_copy(
                        row[:, 1:1 + RW].rearrange("p (h r) -> p h r", h=H)[:, :, 1:1 + n],
                        small[0:1, at:at + RW].rearrange("p (h r) -> p h r", h=H)[:, :, 1:1 + n]),
                        [st["firsts"], st.get("outs"), st.get("old"), *z]))
                both.append(dve.do(lambda e: e.tensor_tensor_scan(
                    out_f[:, 1:1 + RW], singles[:, j, 0:RW], row_f[:, 1:1 + RW], -BIG, ALU.add, ALU.max),
                    [*both, z3, st.get("across")]))
                st["outs"] = dve.do(lambda e: e.tensor_tensor_scan(
                    out_b[:, 1:2 + RW][:, ::-1], singles[:, j, :][:, ::-1], row_b[:, 1:2 + RW][:, ::-1], -BIG,
                    ALU.add, ALU.max), [*both, z4])
                st["fs"] = both[-1]
            elif step == 4:
                m = pe.do(lambda e: e.transpose(back[:, P:P + 1], out_f[0:1, 0:RW], ident[0:1, 0:1]),
                          [st["outs"], st["fs"], st.get("ends"), st.get("exc")])
                st["across"] = pe.do(lambda e: e.transpose(back[:, P + 1:P + 2], out_b[0:1, 2:2 + RW], ident[0:1, 0:1]), [m])
            elif step == 5:
                st["ends"] = dve.do(lambda e: e.tensor_copy(ends[:], back[:, P:P + 2]), [st["across"], st.get("mx")])
                m = forward(fw, lrj, j, ends[:, 0:1], [st["ends"], st["mx0"]])
                st["mx"] = pen_read[j] = backward(mx, fw[:], j, ends[:, 1:2], [m, st["firsts"]])
            elif step == 6:
                m = st["exd"] = lr_read[j] = dve.do(
                    lambda e: e.tensor_tensor(lrj, lrj, mx[:], ALU.subtract), [st["mx"]])
                lr_read[j] = st["exp"] = act.do(lambda e: e.activation(lrj, lrj, ACT.Exp), [m])
                m = pe.do(lambda e: e.transpose(small[0:1, 0:RW], mx[:, 0:1], ident[:]), [st["mx"], *[st["outs"]]])
                st["edge_rows"] = pe.do(lambda e: e.transpose(small[0:1, RW:2 * RW], mx[:, P - 1:P], ident[:]), [m])
            elif step == 7:
                m = pe.do(lambda e: e.transpose(back[:, 0:P], lrj, ident[:]), [st["exp"], st.get("exc"), st["ends"]])
                lr_read[j] = m
                st["exc"] = ex_ready[j] = act.do(lambda e: e.activation(
                    ex[:, j % 2, :, :].rearrange("p h r -> p (h r)"), back[:, 0:P], ACT.Copy), [m, ex_read.get(j - 2)])
                first = small[0:1, 0:RW].rearrange("p (h r) -> p h r", h=H)[:, :, 1]
                final = small[0:1, RW:2 * RW].rearrange("p (h r) -> p h r", h=H)[:, :, n]
                m = dve.do(lambda e: e.tensor_tensor(scale[:, j % 2, :], old[:], first, ALU.subtract),
                           [st["edge_rows"], z5, scaled.get(j - 2), st.get("old")])
                st["scale", j] = act.do(lambda e: e.activation(scale[:, j % 2, :], scale[:, j % 2, :], ACT.Exp), [m])
                m = dve.do(lambda e: e.tensor_copy(old[:], final), [m])
                st["small"] = st["old"] = dve.do(lambda e: e.tensor_copy(
                    row_f[:, 1:1 + RW].rearrange("p (h r) -> p h r", h=H)[:, :, 0], final), [m, st["fs"]])

        m_mask, m_w = {}, {}

        def weigh(i):
            j, r, u = i // BATCH, i % BATCH + 1, i % sums.RING
            ww = ex[:, j % 2, :, r]
            m_mask[i] = sums.make_mask(i)
            v_read[i] = dve.do(lambda e: e.tensor_tensor(
                sums.vals[:, u, 0:D].rearrange("p (h c) -> p h c", h=H),
                vj[:, i % NV, :].rearrange("p (h c) -> p h c", h=H),
                ww.unsqueeze(2).to_broadcast([P, H, C]), ALU.mult),
                [ex_ready[j], v_written[i], sums.product.get(i - sums.RING)])
            m_w[i] = ex_read[j] = act.do(lambda e: e.activation(
                sums.vals[:, u, D:VALS], ww, ACT.Copy), [sums.product.get(i - sums.RING), v_read[i]])

        def sum_up(i):
            j = i // BATCH
            if i % BATCH == 0 and i > 0:
                m = scaled[j] = sums.carry(i, [v_read[i], m_w[i], st["scale", j]], scale=scale[:, j % 2, :])
            else:
                m = sums.carry(i, [v_read[i], m_w[i]])
            sums.sum(i, [m_mask[i], m])

        for c in range(NE - 1):
            load_attrs(c)
        todo, begin = {}, 0
        for j in range(batches):
            begin = max(min(T, (j + 1) * BATCH), begin + 8)
            for step in range(8):
                todo.setdefault(begin + step, []).append((j, step))
        AHEAD = 4
        for i in range(AHEAD):
            gather(i)
        edge_product(0)
        for i in range(T + LAG + 2):
            if i < T:
                if i % CH == 0 and i // CH + NE - 1 < -(-T // CH):
                    load_attrs(i // CH + NE - 1)
                if i % BATCH == 0:
                    penalties(i // BATCH)
                if i + AHEAD < T:
                    gather(i + AHEAD)
                if i + 1 < T:
                    edge_product(i + 1)
                logits(i)
            for j, step in todo.get(i, ()):
                setup_step(j, step)
            if 0 <= i - LAG < T:
                weigh(i - LAG)
            if 0 <= i - LAG - 1 < T:
                sum_up(i - LAG - 1)
            if 0 <= i - LAG - 2:
                sums.keep(i - LAG - 2)
        sums.finish()



class NodeTools:
    def __init__(self, ph, k):
        self.ph, self.k = ph, k
        self.stats = ph.sb("stats", [P, 2, 6])
        self.mv = ph.sb("mv", [P, 2, 2])
        self.rs = ph.sb("rs", [P, 2])
        self.eps = ph.sb("eps", [P, 1])
        self.eps_ok = ph.dve.do(lambda e: e.memset(self.eps[:], LN_EPS))
        self.read = {}

    def layernorm(self, b, out, x, after):
        dve, act, u = self.ph.dve, self.ph.act, b % 2
        m = dve.do(lambda e: e.bn_stats(self.stats[:, u, :], x), [*after, self.read.get(b - 2)])
        m1 = dve.do(lambda e: e.bn_aggr(self.mv[:, u, :], self.stats[:, u, :]), [m])
        m = act.do(lambda e: e.activation(self.rs[:, u:u + 1], self.mv[:, u, 1:2], ACT.Sqrt, bias=self.eps[:, 0:1]),
                   [m1, self.eps_ok])
        m = dve.do(lambda e: e.reciprocal(self.rs[:, u:u + 1], self.rs[:, u:u + 1]), [m])
        self.read[b] = dve.do(lambda e: e.tensor_scalar(
            out, x, self.mv[:, u, 0:1], self.rs[:, u:u + 1], ALU.subtract, ALU.mult), [m, m1])
        return self.read[b]


class Turn:

    def __init__(self, ph, k, name):
        self.ph, self.k = ph, k
        self.psum = ph.psum(f"{name}_turn")
        self.cols = ph.sb(f"{name}_cols", [P, 2, KD, P])
        self.copied, self.used = {}, {}

    def __call__(self, b, x, after):
        ph, u = self.ph, b % 2
        for a in range(KD):
            m = ph.pe.do(lambda e, a=a: e.transpose(
                self.psum[:, a * P:(a + 1) * P], x[:, a * P:(a + 1) * P], self.k["ident"][:]),
                [*after, self.copied.get(b - 1)])
        self.copied[b] = ph.act.do(lambda e: e.activation(
            self.cols[:, u, :, :].rearrange("p a n -> p (a n)"), self.psum[:, 0:KD * P], ACT.Copy),
            [m, self.used.get(b - 2)])
        return self.copied[b]


class Project:

    def __init__(self, ph, k, s, t, conv, turn, tables):
        self.ph, self.turn, self.tables = ph, turn, tables
        self.w = ph.sb("w_proj", [P, KD, 4 * D])
        self.bias = ph.sb("b_proj", [P, 4 * D])
        self.psum = [ph.psum("proj0"), ph.psum("proj1")]
        self.rows = ph.sb("proj_rows", [P, 2, 4 * D])
        self.stores = ph.slots("proj", 2)
        load = ph.slots("proj_w", 1)[0]
        ph.sp.dma(lambda e: e.dma_start(self.w[:], t[f"w_proj{conv}"]), load)
        self.got = ph.sp.dma(lambda e: e.dma_start(self.bias[:], t[f"b_proj{conv}"].to_broadcast([P, 4 * D])), load)
        self.added, self.stored = {}, {}

    def __call__(self, b, cols_ready):
        ph, u = self.ph, b % 2
        kv, qs = self.tables
        for half in range(2):
            cs = slice(half * 2 * D, (half + 1) * 2 * D)
            for a in range(KD):
                m = ph.pe.do(lambda e, a=a, cs=cs, half=half: e.matmul(
                    self.psum[half][:, 0:2 * D], self.turn.cols[:, u, a, :], self.w[:, a, cs],
                    start=(a == 0), stop=(a == KD - 1)), [cols_ready, self.got, self.added.get((b - 1, half))])
            self.turn.used[b] = m
            self.added[b, half] = ph.dve.do(lambda e, cs=cs, half=half: e.tensor_tensor(
                self.rows[:, u, cs], self.psum[half][:, 0:2 * D], self.bias[:, cs], ALU.add),
                [m, self.stored.get(b - 2)])
        r = slice(b * P, (b + 1) * P)
        ph.sp.dma(lambda e: e.dma_start(kv[r, :], self.rows[:, u, 0:2 * D]), self.stores[u], [self.added[b, 0]])
        ph.sp.dma(lambda e: e.dma_start(qs[0][r, :], self.rows[:, u, 2 * D:3 * D]), self.stores[u], [self.added[b, 1]])
        self.stored[b] = ph.sp.dma(lambda e: e.dma_start(qs[1][r, :], self.rows[:, u, 3 * D:4 * D]), self.stores[u])

    def finish(self):
        self.ph.sp.hold([(x.sem, x.count) for x in self.stores])


def gather_sums(ph, k, s, width, table, n=3):
    buf = ph.sb("agg", [P, n, width])
    slots = ph.slots("agg", n)
    marks, read = {}, {}

    def fetch(b):
        if b < s.blocks:
            marks[b] = ph.pool.dma(lambda e: e.indirect_dma_start(
                out=buf[:, b % n, :], out_offset=None, **rows_of(table, k["last_row"][:, b:b + 1])),
                slots[b % n], [read.get(b - n)])

    return buf, marks, read, fetch


def node_pass_resnorm(nc, k, t, s, sums_table, x1_table, tables):
    with Phase(nc, "n0") as ph:
        pe, dve, act, sp = ph.pe, ph.dve, ph.act, ph.sp
        tools = NodeTools(ph, k)
        agg, agg_got, agg_read, fetch = gather_sums(ph, k, s, D, sums_table)
        w12 = ph.sb("w12", [P, 2, KD, D])
        bias = ph.sb("bias", [P, 2, D])
        NX = 4
        x = ph.sb("x", [P, NX, D])
        xt = ph.sb("xt", [P, NX, KD, P])
        y = ph.sb("y", [P, 2, D])
        nb = ph.sb("nb", [P, 2, D])
        o = ph.sb("o", [P, 2, D])
        o2 = ph.sb("o2", [P, 2, D])
        x1 = ph.sb("x1", [P, 3, D])
        ss = ph.sb("ss", [P, 2])
        lin = [ph.psum("lin0"), ph.psum("lin1")]
        turn_y, turn_x = Turn(ph, k, "y"), Turn(ph, k, "x")
        project = Project(ph, k, s, t, 1, turn_x, tables)
        load_w = ph.slots("w", 1)[0]
        sp.dma(lambda e: e.dma_start(w12[:, 0, :, :], t["w1"]), load_w)
        sp.dma(lambda e: e.dma_start(w12[:, 1, :, :], t["w2"]), load_w)
        sp.dma(lambda e: e.dma_start(bias[:, 0, :], t["b1"].to_broadcast([P, D])), load_w)
        m_w = sp.dma(lambda e: e.dma_start(bias[:, 1, :], t["b2"].to_broadcast([P, D])), load_w)
        m_bias = dve.do(lambda e: e.tensor_tensor(bias[:, 0, :], bias[:, 0, :], bias[:, 1, :], ALU.add), [m_w])
        got_x, stores = ph.slots("x", NX), ph.slots("x1", 3)
        x_mark, x_read, lin_read, lin_done, x1_done, x1_stored, o_read = {}, {}, {}, {}, {}, {}, {}

        def load(b):
            if b < s.blocks:
                u = b % NX
                sp.dma(lambda e: e.dma_start(x[:, u, :], t["x_rows"][b * P:(b + 1) * P, :]), got_x[u],
                       [x_read.get(b - NX), lin_done.get(b - NX)])
                x_mark[b] = sp.dma(lambda e: e.dma_start(xt[:, u, :, :], t["x_cols"][:, :, b * P:(b + 1) * P]), got_x[u])
                fetch(b)

        def first(b):
            u, v = b % 2, b % 3
            m = dve.do(lambda e: e.tensor_scalar(nb[:, u, :], agg[:, v, :], k["has_edge"][:, b:b + 1], None, ALU.mult),
                       [agg_got[b]])
            agg_read[b] = m
            m1 = dve.do(lambda e: e.tensor_tensor(y[:, u, :], nb[:, u, :], x[:, b % NX, :], ALU.mult), [m, x_mark[b], turn_y.copied.get(b - 2)])
            m1 = dve.do(lambda e: e.tensor_tensor(y[:, u, :], y[:, u, :], nb[:, u, :], ALU.add), [m1])
            cols = turn_y(b, y[:, u, :], [m1])
            for a in range(KD):
                pe.do(lambda e, a=a: e.matmul(lin[u][:, 0:D], xt[:, b % NX, a, :], w12[:, 0, a, :], start=(a == 0), stop=False),
                      [x_mark[b], m_w, lin_read.get(b - 2)])
            for a in range(KD):
                m = pe.do(lambda e, a=a: e.matmul(lin[u][:, 0:D], turn_y.cols[:, u, a, :], w12[:, 1, a, :],
                                                  start=False, stop=(a == KD - 1)), [cols])
            lin_done[b] = turn_y.used[b] = m

        def second(b):
            u, v = b % 2, b % 3
            m = lin_read[b] = dve.do(lambda e: e.tensor_tensor(o[:, u, :], lin[u][:, 0:D], bias[:, 0, :], ALU.add),
                                     [lin_done[b], m_bias, o_read.get(b - 2)])
            m = dve.do(lambda e: e.scalar_tensor_tensor(
                o2[:, u, :], o[:, u, :], LEAKY, o[:, u, :], ALU.mult, ALU.max), [m, o_read.get(b - 2)])
            q = act.do(lambda e: e.activation(o[:, u, :], o2[:, u, :], ACT.Square, accum_out=ss[:, u:u + 1]), [m])
            q = act.do(lambda e: e.activation(ss[:, u:u + 1], ss[:, u:u + 1], ACT.Sqrt), [q])
            q = dve.do(lambda e: e.tensor_scalar(ss[:, u:u + 1], ss[:, u:u + 1], NORM_EPS, None, ALU.max), [q])
            q = dve.do(lambda e: e.reciprocal(ss[:, u:u + 1], ss[:, u:u + 1]), [q])
            m = x_read[b] = dve.do(lambda e: e.scalar_tensor_tensor(
                o[:, u, :], o2[:, u, :], ss[:, u:u + 1], x[:, b % NX, :], ALU.mult, ALU.add), [q])
            m = x1_done[b] = o_read[b] = tools.layernorm(b, x1[:, v, :], o[:, u, :], [m, x1_stored.get(b - 3), turn_x.copied.get(b - 3)])
            x1_stored[b] = sp.dma(lambda e: e.dma_start(x1_table[b * P:(b + 1) * P, :], x1[:, v, :]), stores[v], [m])

        for b in range(2):
            load(b)
        for b in range(s.blocks + 2):
            load(b + 2)
            if b < s.blocks:
                first(b)
            if 0 <= b - 1 < s.blocks:
                second(b - 1)
            if 0 <= b - 2:
                project(b - 2, turn_x(b - 2, x1[:, (b - 2) % 3, :], [x1_done[b - 2]]))
        project.finish()
        sp.hold([(x.sem, x.count) for x in stores])


def conv_rows(ph, k, s, sums_table, skip_table):
    agg, agg_got, agg_read, fetch = gather_sums(ph, k, s, VALS, sums_table)
    skip = ph.sb("skip", [P, 3, D])
    got = ph.slots("skip", 3)
    rec = ph.sb("rec", [P, 2, H])
    rows = ph.sb("rows", [P, 2, D])
    marks, read, used = {}, {}, {}

    def load(b):
        if b < s.blocks:
            fetch(b)
            marks[b] = ph.sp.dma(lambda e: e.dma_start(skip[:, b % 3, :], skip_table[b * P:(b + 1) * P, :]),
                                 got[b % 3], [read.get(b - 3)])

    def rows_ready(b):
        dve, u, v = ph.dve, b % 2, b % 3
        m = dve.do(lambda e: e.tensor_scalar(rec[:, u, :], agg[:, v, D:VALS], SUM_EPS, None, ALU.add), [agg_got[b]])
        m = dve.do(lambda e: e.reciprocal(rec[:, u, :], rec[:, u, :]), [m])
        m = dve.do(lambda e: e.tensor_scalar(rec[:, u, :], rec[:, u, :], k["has_edge"][:, b:b + 1], None, ALU.mult), [m])
        m = agg_read[b] = dve.do(lambda e: e.tensor_tensor(
            rows[:, u, :].rearrange("p (h c) -> p h c", h=H), agg[:, v, 0:D].rearrange("p (h c) -> p h c", h=H),
            rec[:, u, :].unsqueeze(2).to_broadcast([P, H, C]), ALU.mult), [m, used.get(b - 2)])
        m = read[b] = dve.do(lambda e: e.tensor_tensor(rows[:, u, :], rows[:, u, :], skip[:, v, :], ALU.add), [m, marks[b]])
        return m

    return load, rows, rows_ready, used


def node_pass_hidden(nc, k, t, s, sums_table, skip_table, tables):
    with Phase(nc, "n1") as ph:
        load, rows, rows_ready, used = conv_rows(ph, k, s, sums_table, skip_table)
        turn = Turn(ph, k, "h")
        project = Project(ph, k, s, t, 2, turn, tables)
        done = {}
        for b in range(2):
            load(b)
        for b in range(s.blocks + 1):
            load(b + 2)
            if b < s.blocks:
                m = rows_ready(b)
                done[b] = ph.dve.do(lambda e, b=b: e.tensor_scalar(
                    rows[:, b % 2, :], rows[:, b % 2, :], 0.0, None, ALU.max), [m])
            if b >= 1:
                used[b - 1] = turn(b - 1, rows[:, (b - 1) % 2, :], [done[b - 1]])
                project(b - 1, used[b - 1])
        project.finish()


def node_pass_last(nc, k, t, s, sums_table, skip_table, x1_table, out):
    with Phase(nc, "n2") as ph:
        tools = NodeTools(ph, k)
        load, rows, rows_ready, used = conv_rows(ph, k, s, sums_table, skip_table)
        x1 = ph.sb("x1", [P, 3, D])
        y = ph.sb("y", [P, 2, D])
        got, stores = ph.slots("x1", 3), ph.slots("out", 2)
        marks, read, stored = {}, {}, {}

        def load_all(b):
            load(b)
            if b < s.blocks:
                marks[b] = ph.sp.dma(lambda e: e.dma_start(x1[:, b % 3, :], x1_table[b * P:(b + 1) * P, :]),
                                     got[b % 3], [read.get(b - 3)])

        for b in range(2):
            load_all(b)
        for b in range(s.blocks):
            load_all(b + 2)
            u, n = b % 2, min(P, s.nodes - b * P)
            m = rows_ready(b)
            m = read[b] = ph.dve.do(lambda e, b=b, u=u: e.tensor_tensor(
                rows[:, u, :], rows[:, u, :], x1[:, b % 3, :], ALU.add), [m, marks[b]])
            m = used[b] = tools.layernorm(b, y[:, u, :], rows[:, u, :], [m, stored.get(b - 2)])
            stored[b] = ph.sp.dma(lambda e, b=b, u=u, n=n: e.dma_start(out[b * P:b * P + n, :], y[0:n, u, :]),
                                  stores[u], [m])
        ph.sp.hold([(x.sem, x.count) for x in stores])


def build(nc, t, s, out):
    def scratch(name, shape):
        return nc.dram_tensor(name, shape, F32, kind="Internal").ap()

    slots = s.tiles * P
    sums0 = scratch("sums0", [slots, D])
    sums = [scratch(f"sums{c}", [slots, VALS]) for c in (1, 2)]
    x1 = scratch("x1_rows", [s.rows, D])
    kv = [scratch(f"kv{c}", [s.rows, 2 * D]) for c in (1, 2)]
    q = [scratch(f"q{c}", [s.rows, D]) for c in (1, 2)]
    skip = [scratch(f"skip{c}", [s.rows, D]) for c in (1, 2)]
    with ExitStack() as keep:
        k = constants(nc, keep, t, s)
        singles = single_rows(nc, keep, t, s)
        edge_pass_weighted(nc, k, t, s, sums0)
        node_pass_resnorm(nc, k, t, s, sums0, x1, (kv[0], (q[0], skip[0])))
        edge_pass_attention(nc, "e1", k, t, s, t["w_edge1"], kv[0], q[0], singles, sums[0])
        node_pass_hidden(nc, k, t, s, sums[0], skip[0], (kv[1], (q[1], skip[1])))
        edge_pass_attention(nc, "e2", k, t, s, t["w_edge2"], kv[1], q[1], singles, sums[1])
        node_pass_last(nc, k, t, s, sums[1], skip[1], x1, out)



def lay_out(x, src, dst, edge_attr_194, edge_weight, L0_gnn_W1, L0_gnn_b1, L0_gnn_W2, L0_gnn_b2, **conv):
    n, e, f = x.shape[0], src.shape[0], edge_attr_194.shape[1]
    s = Shapes(n, e, f)

    def slots(a, front, behind):
        line = np.full(s.cols, behind, a.dtype)
        line[0], line[1:1 + e] = front, a
        return np.ascontiguousarray(line[np.arange(s.tiles)[:, None] * OWN + np.arange(P)[None, :]])

    def halves(w, rows):
        full = np.zeros((rows * -(-w.shape[0] // rows), w.shape[1]), w.dtype)
        full[:w.shape[0]] = w
        return np.ascontiguousarray(full.reshape(-1, rows, w.shape[1]).transpose(1, 0, 2))

    dst_rows = slots(dst, s.front, s.behind)
    dst_next = dst_rows.copy()
    dst_next[:, 0] = dst_rows[:, 1]
    x_rows = np.zeros((s.rows, x.shape[1]), x.dtype)
    x_rows[:n] = x
    attr = np.zeros((2 * s.ka, s.cols), edge_attr_194.dtype)
    attr[:f, 1:1 + e] = edge_attr_194.T
    t = {
        "dst_rows": dst_rows,
        "dst_cols": np.ascontiguousarray(dst_rows.T),
        "dst_next_cols": np.ascontiguousarray(dst_next.T),
        "src_cols": np.ascontiguousarray(slots(src, 0, 0).T),
        "weight_cols": np.ascontiguousarray(slots(edge_weight, 0, 0).T),
        "x_rows": x_rows,
        "x_cols": halves(x_rows.T, P),
        "attr_cols": np.ascontiguousarray(attr.reshape(2, s.ka, s.cols).transpose(1, 0, 2)),
        "w1": halves(L0_gnn_W1.T, P), "w2": halves(L0_gnn_W2.T, P),
        "b1": L0_gnn_b1[None, :], "b2": L0_gnn_b2[None, :],
    }
    for c in (1, 2):
        g = lambda name: conv[f"L1_gnn_{name}{c}"]
        t[f"w_proj{c}"] = halves(np.concatenate([g("Wk"), g("Wv"), g("Wq"), g("Ws")], axis=1), P)
        t[f"b_proj{c}"] = np.concatenate([g("bk"), g("bv"), g("bq"), g("bs")])[None, :]
        t[f"w_edge{c}"] = halves(g("We"), s.ka)
    return s, {name: np.ascontiguousarray(a) for name, a in t.items()}


def kernel(**inputs):
    import concourse.bacc as _bacc
    from concourse.bass_utils import run_bass_kernel_spmd as _run

    s, arrays = lay_out(**{name: np.asarray(a) for name, a in inputs.items()})
    nc = _bacc.Bacc("TRN2", target_bir_lowering=False, num_devices=1)
    t = {name: nc.dram_tensor(name, a.shape, mybir.dt.from_np(a.dtype), kind="ExternalInput").ap()
         for name, a in arrays.items()}
    out = nc.dram_tensor("out", (s.nodes, D), F32, kind="ExternalOutput").ap()
    build(nc, t, s, out)
    r = _run(nc, [arrays], core_ids=[0])
    return r.results[0]["out"]
```

```python
from contextlib import ExitStack

import numpy as np

import concourse.bass as bass
from concourse import mybir

P = 128
OWN = P - 1
D = 256
H = 4
C = D // H
KD = D // P
BATCH = 30
ROWS = 32
VALS = D + H
BIG = float(2.0 ** 100)
LEAKY = 0.2
NORM_EPS = 1e-12
LN_EPS = 1e-5
SUM_EPS = 1e-16

F32 = mybir.dt.float32
BF16 = mybir.dt.bfloat16
I32 = mybir.dt.int32
ALU = mybir.AluOpType
ACT = mybir.ActivationFunctionType


class Shapes:
    def __init__(self, nodes, edges, attrs):
        self.nodes, self.edges, self.attrs = nodes, edges, attrs
        self.tiles = -(-edges // OWN)
        self.blocks = -(-nodes // P)
        self.rows = self.blocks * P
        self.cols = self.tiles * OWN + 1
        self.ka = -(-attrs // 32) * 16
        self.front, self.behind = self.rows - 2, self.rows - 1
        assert nodes <= self.rows - 2 and BATCH % 2 == 0 and BATCH < ROWS


class Lane:

    def __init__(self, sem):
        self.sem, self.count, self.program, self.seen = sem, 0, [], {}

    def _add(self, build, after, sem, step):
        waits = []
        for mark in after:
            if mark is not None and self.seen.get(id(mark[0]), 0) < mark[1]:
                self.seen[id(mark[0])] = mark[1]
                waits.append(mark)
        self.program.append((waits, build, sem, step))

    def do(self, build, after=()):
        self._add(build, after, self.sem, 1)
        self.count += 1
        return self.sem, self.count

    def dma(self, build, slot, after=()):
        self._add(build, after, slot.sem, 16)
        slot.count += 16
        return slot.sem, slot.count

    def hold(self, after):
        self._add(None, after, None, 0)

    def play(self, eng):
        for waits, build, sem, step in self.program:
            for s, value in waits:
                eng.wait_ge(s, value)
            if build is not None:
                build(eng).then_inc(sem, step)


class Slot:
    def __init__(self, sem):
        self.sem, self.count = sem, 0


class Phase:

    def __init__(self, nc, name):
        self.nc, self.name, self.stack = nc, name, ExitStack()

    def __enter__(self):
        self.stack.__enter__()
        self.pe, self.dve, self.act, self.pool, self.sp = (
            Lane(self.sem(n)) for n in ("pe", "dve", "act", "pool", "sp"))
        return self

    def sb(self, name, shape, dtype=F32):
        return self.stack.enter_context(self.nc.sbuf_tensor(f"{self.name}_{name}", shape, dtype))

    def psum(self, name):
        return self.stack.enter_context(self.nc.psum_tensor(f"{self.name}_{name}", [P, 512], F32))

    def sem(self, name):
        return self.stack.enter_context(self.nc.semaphore(f"{self.name}_{name}_done"))

    def slots(self, name, n):
        return [Slot(self.sem(f"{name}{i}")) for i in range(n)]

    def __exit__(self, kind, *rest):
        if kind is None:
            with self.nc.Block() as block:
                for start, lane in ((block.tensor, self.pe), (block.vector, self.dve), (block.scalar, self.act),
                                    (block.gpsimd, self.pool), (block.sync, self.sp)):
                    start(lane.play)
        return self.stack.__exit__(kind, *rest)


def rows_of(table, index):
    return dict(in_=table, in_offset=bass.IndirectOffsetOnAxis(ap=index, axis=0))



def constants(nc, keep, t, s):
    k = {}

    def sb(name, shape, dtype=F32):
        k[name] = keep.enter_context(nc.sbuf_tensor(name, shape, dtype))
        return k[name]

    ident = sb("ident", [P, P])
    slot_of = sb("slot_of", [P, P])
    upto = sb("upto", [P, P])
    upto_open = sb("upto_open", [P, P])
    run_end = sb("run_end", [P, s.tiles])
    link_end = sb("link_end", [P, s.tiles])
    src = sb("src_sb", [P, s.tiles], I32)
    dst = sb("dst_sb", [P, s.tiles], I32)
    weight = sb("weight_sb", [P, s.tiles])
    last_row = sb("last_row", [P, s.blocks], I32)
    has_edge = sb("has_edge", [P, s.blocks])

    groups = -(-s.tiles // P)
    with Phase(nc, "setup") as ph:
        pe, dve, pool, sp = ph.pe, ph.dve, ph.pool, ph.sp
        load = ph.slots("load", 5)
        got_src = sp.dma(lambda e: e.dma_start(src[:], t["src_cols"]), load[0])
        got_dst = sp.dma(lambda e: e.dma_start(dst[:], t["dst_cols"]), load[0])
        got_w = sp.dma(lambda e: e.dma_start(weight[:], t["weight_cols"]), load[0])

        z = pool.do(lambda e: e.memset(ident[:], 0.0))
        m_id = pool.do(lambda e: e.affine_select(
            out=ident[:], in_=ident[:], compare_op=ALU.not_equal, fill=1.0, base=0,
            pattern=[[-1, P]], channel_multiplier=1), [z])
        iota = ph.sb("iota", [P, P])
        m_io = pool.do(lambda e: e.iota(iota[:], pattern=[[1, P]], base=0, channel_multiplier=0,
                                        allow_small_or_imprecise_dtypes=True))
        a = pool.do(lambda e: e.iota(slot_of[:], pattern=[[1, P]], base=0, channel_multiplier=0,
                                     allow_small_or_imprecise_dtypes=True))
        a = pool.do(lambda e: e.memset(slot_of[:, 0:1], float(P - 1)), [a])
        b = pool.do(lambda e: e.memset(upto[:], 1.0))
        b = pool.do(lambda e: e.affine_select(
            out=upto[:], in_=upto[:], compare_op=ALU.is_ge, fill=0.0, base=0,
            pattern=[[1, P]], channel_multiplier=-1), [b])
        b = pool.do(lambda e: e.memset(upto[:, 0:1], 1.0), [b])

        c = pool.do(lambda e: e.memset(upto_open[:], 1.0))
        c = pool.do(lambda e: e.affine_select(
            out=upto_open[:], in_=upto_open[:], compare_op=ALU.is_ge, fill=0.0, base=0,
            pattern=[[1, P]], channel_multiplier=-1), [c])
        c = pool.do(lambda e: e.memset(upto_open[:, 0:1], 1.0), [c])
        c = pool.do(lambda e: e.memset(upto_open[0:1, :], 0.0), [c])

        d_int = [ph.sb(f"d_int{i}", [P, P], I32) for i in range(2)]
        d_f = [ph.sb(f"d_f{i}", [P, P]) for i in range(2)]
        same = [ph.sb(f"same{i}", [P, P]) for i in range(2)]
        ends = [ph.sb(f"ends{i}", [P, P]) for i in range(2)]
        turned = ph.psum("turned")
        zero = [dve.do(lambda e, x=x: e.memset(x[:], 0.0)) for x in same + ends]
        same_m = zero[:2]
        copied = [None, None]
        pe_read = [zero[2], zero[3]]
        for g in range(groups):
            n, u = min(P, s.tiles - g * P), g % 2
            m = sp.dma(lambda e, g=g, n=n, u=u: e.dma_start(d_int[u][0:n, :], t["dst_rows"][g * P:g * P + n, :]),
                       load[1 + u], [copied[u]])
            m = copied[u] = dve.do(lambda e, n=n, u=u: e.tensor_copy(d_f[u][0:n, :], d_int[u][0:n, :]), [m, same_m[u]])
            m = same_m[u] = dve.do(lambda e, n=n, u=u: e.tensor_tensor(
                same[u][0:n, 0:P - 1], d_f[u][0:n, 1:P], d_f[u][0:n, 0:P - 1], ALU.is_equal), [m, same_m[u]])
            m = dve.do(lambda e, n=n, u=u: e.tensor_tensor_scan(
                ends[u][0:n, ::-1], same[u][0:n, ::-1], iota[0:n, ::-1], 0.0, ALU.mult, ALU.max),
                [m, m_io, pe_read[u]])
            m = pe_read[u] = pe.do(lambda e, n=n, u=u: e.transpose(
                turned[:, u * P:u * P + n], ends[u][0:n, :], ident[0:n, 0:n]), [m, m_id])
            dve.do(lambda e, g=g, n=n, u=u: e.tensor_copy(
                run_end[:, g * P:g * P + n], turned[:, u * P:u * P + n]), [m])
            pe_read[u] = (dve.sem, dve.count)
        goes_on = ph.sb("goes_on", [P, s.tiles])
        spread = ph.psum("spread")
        ends_ready = (dve.sem, dve.count)
        z = dve.do(lambda e: e.memset(link_end[:], -1.0))
        m1 = dve.do(lambda e: e.tensor_scalar(goes_on[:], run_end[:], float(P - 1), None, ALU.is_equal), [ends_ready])
        m = None
        for a in range(1, s.tiles, 512):
            n = min(512, s.tiles - a)
            m = pe.do(lambda e, a=a, n=n: e.matmul(spread[:, 0:n], upto[0:1, :], run_end[0:1, a:a + n],
                                                   start=True, stop=True), [ends_ready, b, m])
            m = dve.do(lambda e, a=a, n=n: e.scalar_tensor_tensor(
                link_end[:, a:a + n], spread[:, 0:n], 1.0, goes_on[:, a - 1:a - 1 + n], ALU.add, ALU.mult), [m, z, m1])
        dve.do(lambda e: e.tensor_scalar(link_end[:, 1:], link_end[:, 1:], -1.0, None, ALU.add), [m])
        sp.hold([got_src, got_dst, got_w])
    return k


def single_rows(nc, keep, t, s):
    batches = -(-s.tiles // BATCH)
    singles = keep.enter_context(nc.sbuf_tensor("singles", [1, batches, H * ROWS + 1], F32))
    with Phase(nc, "single") as ph:
        dve, sp = ph.dve, ph.sp
        ends = ph.sb("ends", [1, 2, s.tiles], I32)
        endf = ph.sb("endf", [1, 2, s.tiles])
        pen = ph.sb("pen", [1, s.tiles])
        load = ph.slots("load", 1)[0]
        sp.dma(lambda e: e.dma_start(ends[:, 0, :], t["dst_cols"][0:1, :]), load)
        m = sp.dma(lambda e: e.dma_start(ends[:, 1, :], t["dst_cols"][P - 1:P, :]), load)
        z = dve.do(lambda e: e.memset(singles[:], -BIG))
        m = dve.do(lambda e: e.tensor_copy(endf[:], ends[:]), [m])
        m = dve.do(lambda e: e.tensor_tensor(pen[:], endf[:, 0, :], endf[:, 1, :], ALU.not_equal), [m])
        m = dve.do(lambda e: e.tensor_scalar(pen[:], pen[:], -BIG, None, ALU.mult), [m])
        for j in range(batches):
            n = min(BATCH, s.tiles - j * BATCH)
            for h in range(H):
                dve.do(lambda e, j=j, n=n, h=h: e.tensor_copy(
                    singles[:, j, ROWS * h + 1:ROWS * h + 1 + n], pen[:, j * BATCH:j * BATCH + n]), [m, z])
    return singles



class RunSums:

    GROUP = 4
    PAIRS = 3
    RING = 2 * PAIRS

    def __init__(self, ph, k, s, width, table):
        self.ph, self.k, self.s, self.width, self.table = ph, k, s, width, table
        self.mask = ph.sb("run_mask", [P, self.RING, P])
        self.link = ph.sb("link_mask", [P, self.PAIRS, P])
        self.vals = ph.sb("vals", [P, self.RING, width])
        self.out = [[ph.psum(f"sum{u}{half}") for half in range(2)] for u in range(2)]
        self.rows = ph.sb("sum_rows", [P, 2, self.GROUP, width])
        self.stores = ph.slots("store", 2)
        self.summed = {}
        self.used = {}
        self.evac, self.stored = {}, {}
        self.view = table.rearrange("(t p) c -> p t c", p=P)

    def free(self, i):
        return self.used.get(i // 2 - self.PAIRS)

    def make_masks(self, i):
        k, u, dve = self.k, i % self.RING, self.ph.dve
        upto = k["upto"] if i % 2 == 0 else k["upto_open"]
        m = dve.do(lambda e: e.scalar_tensor_tensor(
            self.mask[:, u, :], k["slot_of"][:], k["run_end"][:, i:i + 1], upto[:], ALU.is_le, ALU.mult),
            [self.free(i)])
        if i % 2 == 0:
            return m
        return dve.do(lambda e: e.tensor_scalar(
            self.link[:, i // 2 % self.PAIRS, :], k["slot_of"][:], k["link_end"][:, i:i + 1], None, ALU.is_le))

    def carry(self, p, after, scale=None):
        act, dve, v = self.ph.act, self.ph.dve, self.vals
        w, u = self.width, 2 * p % self.RING
        if p == 0:
            return dve.do(lambda e: e.memset(v[0:1, u, :], 0.0), after)
        prev = self.out[(p - 1) % 2][1]
        m = act.do(lambda e: e.activation(v[0:1, u, :], prev[0:1, 0:w], ACT.Copy), after + [self.summed[2 * p - 1]])
        if scale is None:
            return m
        row = v[0:1, u, 0:D].rearrange("p (h c) -> p h c", h=H)
        m = dve.do(lambda e: e.tensor_tensor(row, row, scale.unsqueeze(2).to_broadcast([1, H, C]), ALU.mult), [m])
        return dve.do(lambda e: e.tensor_tensor(v[0:1, u, D:w], v[0:1, u, D:w], scale, ALU.mult), [m])

    def sum_first(self, p, after):
        i, out, w, u = 2 * p + 1, self.out[p % 2][1], self.width, (2 * p + 1) % self.RING
        if i < self.s.tiles:
            self.ph.pe.do(lambda e: e.matmul(
                out[:, 0:w], self.mask[:, u, :], self.vals[:, u, :], start=True, stop=False),
                after + [self.evac.get(i - 4)])

    def sum_rest(self, p, after):
        pe, w, u = self.ph.pe, self.width, 2 * p % self.RING
        first, second = self.out[p % 2]
        if 2 * p + 1 < self.s.tiles:
            self.summed[2 * p + 1] = pe.do(lambda e: e.matmul(
                second[:, 0:w], self.link[:, p % self.PAIRS, :], self.vals[:, u, :], start=False, stop=True), after)
        self.summed[2 * p] = self.used[p] = pe.do(lambda e: e.matmul(
            first[:, 0:w], self.mask[:, u, :], self.vals[:, u, :], start=True, stop=True),
            after + [self.evac.get(2 * p - 4)])

    def keep(self, p):
        if p < 0:
            return
        ph, w, grp, end = self.ph, self.width, self.GROUP, min(2 * p + 2, self.s.tiles)
        g = 2 * p // grp
        for i in range(end - 1, 2 * p - 1, -1):
            out = self.out[p % 2][i % 2]
            self.evac[i] = ph.act.do(lambda e, i=i, out=out: e.activation(
                self.rows[:, g % 2, i % grp, :], out[:, 0:w], ACT.Copy), [self.summed[i], self.stored.get(g - 2)])
        if end % grp == 0 or end == self.s.tiles:
            self.stored[g] = ph.sp.dma(lambda e: e.dma_start(
                self.view[:, g * grp:end, :], self.rows[:, g % 2, 0:end - g * grp, :]),
                self.stores[g % 2], [self.evac[2 * p]])

    def finish(self):
        self.ph.sp.hold([(x.sem, x.count) for x in self.stores])


def edge_pass_weighted(nc, k, t, s, table):
    with Phase(nc, "e0") as ph:
        pe, dve, act, pool, sp = ph.pe, ph.dve, ph.act, ph.pool, ph.sp
        NX = 6
        x = ph.sb("x", [P, NX, D])
        got = ph.slots("x", NX)
        sums = RunSums(ph, k, s, D, table)
        ident = k["ident"]

        load = ph.slots("load", 1)[0]
        num = ph.sb("num", [P, s.tiles], I32)
        part = ph.sb("part", [P, s.tiles], I32)
        hi = ph.sb("hi", [P, s.tiles])
        lo = ph.sb("lo", [P, s.tiles])
        iota = ph.sb("iota", [P, P], BF16)
        one_hi = ph.sb("one_hi", [P, 4, s.blocks], BF16)
        one_lo = ph.sb("one_lo", [P, 4, P], BF16)
        count = ph.psum("count")
        m = sp.dma(lambda e: e.dma_start(num[:], t["dst_next_cols"]), load)
        m1 = dve.do(lambda e: e.tensor_scalar(part[:], num[:], P.bit_length() - 1, None, ALU.arith_shift_right), [m])
        m_hi = dve.do(lambda e: e.tensor_copy(hi[:], part[:]), [m1])
        m2 = dve.do(lambda e: e.tensor_scalar(part[:], num[:], P - 1, None, ALU.bitwise_and), [m_hi])
        m_lo = dve.do(lambda e: e.tensor_copy(lo[:], part[:]), [m2])
        m_io = pool.do(lambda e: e.iota(iota[:], pattern=[[1, P]], base=0, channel_multiplier=0,
                                        allow_small_or_imprecise_dtypes=True))
        counted = {}
        weighted, carried, mask, hot = {}, {}, {}, {}
        R = sums.RING
        for i in range(s.tiles + 4):
            if i < s.tiles:
                u = i % NX
                m_x = pool.dma(lambda e, i=i, u=u: e.indirect_dma_start(
                    out=x[:, u, :], out_offset=None, **rows_of(t["x_rows"], k["src_sb"][:, i:i + 1])),
                    got[u], [weighted.get(i - NX)])
                mask[i] = sums.make_masks(i)
                m = dve.do(lambda e, i=i: e.tensor_scalar(one_lo[:, i % 4, :], iota[:], lo[:, i:i + 1], None, ALU.is_equal),
                           [m_lo, m_io, counted.get(i - 4)])
                hot[i] = dve.do(lambda e, i=i: e.tensor_scalar(one_hi[:, i % 4, :], iota[:, 0:s.blocks], hi[:, i:i + 1],
                                                               None, ALU.is_equal), [m_hi, counted.get(i - 4)])
            p = (i - 3) // 2
            if i >= 3 and i % 2 == 1 and 2 * p < s.tiles:
                if p:
                    carried[p] = sums.carry(p, [weighted[2 * p]])
            if i < s.tiles:
                weighted[i] = act.do(lambda e, i=i, u=u: e.activation(
                    sums.vals[:, i % R, :], x[:, u, :], ACT.Copy, scale=k["weight_sb"][:, i:i + 1]), [m_x, sums.free(i)])
            if i >= 3 and i % 2 == 1 and 2 * p < s.tiles:
                if not p:
                    carried[p] = sums.carry(p, [weighted[0]])
                rest = [weighted.get(2 * p + 1), mask.get(2 * p + 1), mask[2 * p], carried[p]]
                sums.sum_first(p, rest[:2])
                sums.sum_rest(p, rest)
                for n in range(2 * p, min(2 * p + 2, s.tiles)):
                    counted[n] = pe.do(lambda e, n=n: e.matmul(
                        count[0:s.blocks, 0:P], one_hi[:, n % 4, :], one_lo[:, n % 4, :],
                        start=(n == 0), stop=(n == s.tiles - 1)), [hot[n]])
                sums.keep(p - 1)
        sums.keep((s.tiles - 1) // 2)
        sums.finish()

        B = s.blocks
        cnt = ph.sb("cnt", [B, P])
        run = ph.sb("run", [B, P])
        before = ph.sb("before", [B, B])
        has = ph.sb("has", [B, P])
        base = ph.sb("base", [B, 1])
        small = ph.psum("small")
        m_b = pool.do(lambda e: e.memset(before[:], 1.0))
        m_b = pool.do(lambda e: e.affine_select(
            out=before[:], in_=before[:], compare_op=ALU.is_ge, fill=0.0, base=-1,
            pattern=[[1, B]], channel_multiplier=-1), [m_b])
        m = dve.do(lambda e: e.tensor_copy(cnt[:], count[0:B, 0:P]), [counted[s.tiles - 1]])
        m_has = dve.do(lambda e: e.tensor_scalar(has[:], cnt[:], 0.0, None, ALU.is_gt), [m])
        m = dve.do(lambda e: e.tensor_tensor_scan(run[:], cnt[:], cnt[:], 0.0, ALU.add, ALU.bypass), [m])
        m2 = pe.do(lambda e: e.matmul(small[0:B, 0:1], before[:], run[:, P - 1:P], start=True, stop=True), [m, m_b])
        m2 = dve.do(lambda e: e.tensor_copy(base[:], small[0:B, 0:1]), [m2])
        m = dve.do(lambda e: e.tensor_scalar(run[:], run[:], base[:, 0:1], -1.0, ALU.add, ALU.add), [m, m2])
        m = dve.do(lambda e: e.tensor_scalar(run[:], run[:], 0.0, None, ALU.max), [m])
        m = pe.do(lambda e: e.transpose(small[:, 128:128 + B], run[:], ident[0:B, 0:B]), [m, m2])
        m_has = pe.do(lambda e: e.transpose(small[:, 256:256 + B], has[:], ident[0:B, 0:B]), [m_has])
        dve.do(lambda e: e.tensor_copy(k["last_row"][:], small[:, 128:128 + B]), [m_has])
        dve.do(lambda e: e.tensor_copy(k["has_edge"][:], small[:, 256:256 + B]), [m_has])


def edge_pass_attention(nc, name, k, t, s, w_edge, kv_rows, q_rows, singles, table):
    CH = 8
    RUNS_READY = 8
    STEPS = 14
    LAG = BATCH + STEPS
    NV, NKV, NQ, NE = LAG + 4, 8, 8, 3
    ident = k["ident"]
    batches = -(-s.tiles // BATCH)
    T = s.tiles
    with Phase(nc, name) as ph:
        pe, dve, act, pool, sp = ph.pe, ph.dve, ph.act, ph.pool, ph.sp
        sums = RunSums(ph, k, s, VALS, table)
        we = ph.sb("we", [s.ka, 2, D])
        ea = ph.sb("ea", [s.ka, NE, 2, CH * OWN + 1])
        kv = ph.sb("kv", [P, NKV, 2, D])
        q = ph.sb("q", [P, NQ, D])
        kj = ph.sb("kj", [P, 2, D])
        vj = ph.sb("vj", [P, NV, D])
        logit = ph.sb("logit", [P, 2, H, ROWS])
        ex = ph.sb("ex", [P, 2, H, ROWS])
        pe_e = [ph.psum("e0"), ph.psum("e1")]
        back, small = ph.psum("back"), ph.psum("small")
        flat = small[:, 2 * H * ROWS:2 * H * ROWS + P]
        d_int = ph.sb("d_int", [P, 2, P], I32)
        d_f = ph.sb("d_f", [P, P])
        pen = ph.sb("pen", [P, 2, P + 1])
        lr = ph.sb("lr", [P, 2, P])
        fw = ph.sb("fw", [P, P])
        mx = ph.sb("mx", [P, P])
        ends = ph.sb("ends", [P, 2])
        RW = H * ROWS
        row_f = ph.sb("row_f", [1, RW + 2])
        row_b = ph.sb("row_b", [1, RW + 2])
        out_f = ph.sb("out_f", [1, RW + 2])
        out_b = ph.sb("out_b", [1, RW + 2])
        old = ph.sb("old", [1, H])
        scale = ph.sb("scale", [1, 2, H])
        got_kv, got_q, got_ea, got_d = (ph.slots(n, c) for n, c in (("kv", NKV), ("q", NQ), ("ea", NE), ("d", 2)))
        w_slot = ph.slots("w", 1)[0]

        got_w = sp.dma(lambda e: e.dma_start(we[:], w_edge), w_slot)
        z0 = dve.do(lambda e: e.memset(logit[:], 0.0))
        z1 = dve.do(lambda e: e.memset(pen[:], 0.0))
        z2 = dve.do(lambda e: e.memset(row_f[:], -BIG))
        z3 = dve.do(lambda e: e.memset(out_f[:], -BIG))
        z4 = dve.do(lambda e: e.memset(out_b[:], -BIG))
        z5 = dve.do(lambda e: e.memset(old[:], -BIG))

        ea_mark, ea_read, e_done = {}, {}, {}
        kj_read, v_written, v_read, dots = {}, {}, {}, {}
        turned, ex_ready, scaled = {}, {}, {}
        st = {}
        pen_read, lr_read, ex_read = {}, {}, {}

        def load_attrs(c):
            n = min(CH, T - c * CH) * OWN + 1
            ea_mark[c] = sp.dma(lambda e: e.dma_start(
                ea[:, c % NE, :, 0:n], t["attr_cols"][:, :, c * CH * OWN:c * CH * OWN + n]),
                got_ea[c % NE], [ea_read.get(c - NE)])

        def gather(i):
            u, w = i % NKV, i % NQ
            st["kv", i] = pool.dma(lambda e: e.indirect_dma_start(
                out=kv[:, u, :, :].rearrange("p a d -> p (a d)"), out_offset=None,
                **rows_of(kv_rows, k["src_sb"][:, i:i + 1])), got_kv[u], [v_written.get(i - NKV), kj_read.get(i - NKV)])
            st["q", i] = pool.dma(lambda e: e.indirect_dma_start(
                out=q[:, w, :], out_offset=None, **rows_of(q_rows, k["dst_sb"][:, i:i + 1])),
                got_q[w], [dots.get(i - NQ)])

        edge_done = {}

        def edge_product(i):
            c, off = i // CH, (i % CH) * OWN
            for a in range(2):
                m = pe.do(lambda e, a=a: e.matmul(
                    pe_e[i % 2][:, 0:D], ea[:, c % NE, a, off:off + P], we[:, a, :], start=(a == 0), stop=(a == 1)),
                    [ea_mark[c], got_w, v_written.get(i - 2), kj_read.get(i - 2)])
            ea_read[c] = edge_done[i] = m

        def logits(i):
            m, j, r = edge_done[i], i // BATCH, i % BATCH + 1
            mk = kj_read[i] = dve.do(lambda e: e.tensor_tensor(
                kj[:, i % 2, :], kv[:, i % NKV, 0, :], pe_e[i % 2][:, 0:D], ALU.add), [st["kv", i], m, dots.get(i - 2)])
            v_written[i] = dve.do(lambda e: e.tensor_tensor(
                vj[:, i % NV, :], kv[:, i % NKV, 1, :], pe_e[i % 2][:, 0:D], ALU.add), [v_read.get(i - NV)])
            for h in range(H):
                hs = slice(h * C, h * C + C)
                m = dve.do(lambda e, h=h, hs=hs: e.tensor_tensor_reduce(
                    kj[:, i % 2, hs], kj[:, i % 2, hs], q[:, i % NQ, hs], 1.0, 0.0, ALU.mult, ALU.add,
                    logit[:, j % 2, h, r:r + 1]), [mk, st["q", i], z0, turned.get(j - 2)])
            dots[i] = m

        def load_runs(j):
            n = min(BATCH, T - j * BATCH)
            for h in range(H):
                m = sp.dma(lambda e, h=h: e.dma_start(
                    d_int[ROWS * h + 1:ROWS * h + 1 + n, j % 2, :], t["dst_rows"][j * BATCH:j * BATCH + n, :]),
                    got_d[j % 2], [st.get(("d", j - 2)), st["dz"]])
            st["runs", j] = m

        def penalties(j):
            m = st["runs", j]
            m = st["d", j] = dve.do(lambda e: e.tensor_copy(d_f[:], d_int[:, j % 2, :]), [m, st.get(("ne", j - 1))])
            m = st["ne", j] = dve.do(lambda e: e.tensor_tensor(
                pen[:, j % 2, 1:P], d_f[:, 1:P], d_f[:, 0:P - 1], ALU.not_equal), [m, z1, pen_read.get(j - 2)])
            st["pen", j] = dve.do(lambda e: e.tensor_scalar(
                pen[:, j % 2, 1:P], pen[:, j % 2, 1:P], -BIG, None, ALU.mult), [m])

        st["dz"] = dve.do(lambda e: e.memset(d_int[:], 0))

        def forward(out, data, j, initial, after):
            return dve.do(lambda e: e.tensor_tensor_scan(
                out[:], pen[:, j % 2, 0:P], data, initial, ALU.add, ALU.max), after)

        def backward(out, data, j, initial, after):
            return dve.do(lambda e: e.tensor_tensor_scan(
                out[:, ::-1], pen[:, j % 2, 1:P + 1][:, ::-1], data[:, ::-1], initial, ALU.add, ALU.max), after)

        def setup_step(j, step):
            n = min(BATCH, T - j * BATCH)
            last = j * BATCH + n - 1
            lrj = lr[:, j % 2, :]
            if step == 0:
                m = turned[j] = pe.do(lambda e: e.transpose(
                    flat, logit[:, j % 2, :, :].rearrange("p h r -> p (h r)"), ident[:]),
                    [dots[last], st.get("lr"), st.get("small")])
                st["lr"] = act.do(lambda e: e.activation(
                    lrj, flat, ACT.Copy, scale=1.0 / float(np.sqrt(C))), [m, lr_read.get(j - 2)])
            elif step == 1:
                m = forward(fw, lrj, j, -BIG, [st["lr"], st["pen", j], st.get("mx")])
                st["mx0"] = backward(mx, fw[:], j, -BIG, [m, st.get("exd"), st.get("edge_rows")])
            elif step == 2:
                m = pe.do(lambda e: e.transpose(small[0:1, 0:RW], mx[:, P - 1:P], ident[:]), [st["mx0"], st.get("small")])
                st["firsts"] = pe.do(lambda e: e.transpose(small[0:1, RW:2 * RW], mx[:, 0:1], ident[:]), [m])
            elif step == 3:
                both = []
                z = [z2, dve.do(lambda e: e.memset(row_b[:], -BIG), [st.get("outs")])]
                for row, at in ((row_f, 0), (row_b, RW)):
                    both.append(dve.do(lambda e, row=row, at=at: e.tensor_copy(
                        row[:, 1:1 + RW].rearrange("p (h r) -> p h r", h=H)[:, :, 1:1 + n],
                        small[0:1, at:at + RW].rearrange("p (h r) -> p h r", h=H)[:, :, 1:1 + n]),
                        [st["firsts"], st.get("outs"), st.get("old"), *z]))
                both.append(dve.do(lambda e: e.tensor_tensor_scan(
                    out_f[:, 1:1 + RW], singles[:, j, 0:RW], row_f[:, 1:1 + RW], -BIG, ALU.add, ALU.max),
                    [*both, z3, st.get("across")]))
                st["outs"] = dve.do(lambda e: e.tensor_tensor_scan(
                    out_b[:, 1:2 + RW][:, ::-1], singles[:, j, :][:, ::-1], row_b[:, 1:2 + RW][:, ::-1], -BIG,
                    ALU.add, ALU.max), [*both, z4])
                st["fs"] = both[-1]
            elif step == 4:
                m = pe.do(lambda e: e.transpose(back[:, P:P + 1], out_f[0:1, 0:RW], ident[0:1, 0:1]),
                          [st["outs"], st["fs"], st.get("ends"), st.get("exc")])
                st["across"] = pe.do(lambda e: e.transpose(back[:, P + 1:P + 2], out_b[0:1, 2:2 + RW], ident[0:1, 0:1]), [m])
            elif step == 5:
                st["ends"] = dve.do(lambda e: e.tensor_copy(ends[:], back[:, P:P + 2]), [st["across"], st.get("mx")])
                m = forward(fw, lrj, j, ends[:, 0:1], [st["ends"], st["mx0"]])
                st["mx"] = pen_read[j] = backward(mx, fw[:], j, ends[:, 1:2], [m, st["firsts"]])
            elif step == 6:
                m = st["exd"] = lr_read[j] = dve.do(
                    lambda e: e.tensor_tensor(lrj, lrj, mx[:], ALU.subtract), [st["mx"]])
                lr_read[j] = st["exp"] = act.do(lambda e: e.activation(lrj, lrj, ACT.Exp), [m])
                m = pe.do(lambda e: e.transpose(small[0:1, 0:RW], mx[:, 0:1], ident[:]), [st["mx"], *[st["outs"]]])
                st["edge_rows"] = pe.do(lambda e: e.transpose(small[0:1, RW:2 * RW], mx[:, P - 1:P], ident[:]), [m])
            elif step == 7:
                m = pe.do(lambda e: e.transpose(back[:, 0:P], lrj, ident[:]), [st["exp"], st.get("exc"), st["ends"]])
                lr_read[j] = m
                st["exc"] = ex_ready[j] = act.do(lambda e: e.activation(
                    ex[:, j % 2, :, :].rearrange("p h r -> p (h r)"), back[:, 0:P], ACT.Copy), [m, ex_read.get(j - 2)])
                first = small[0:1, 0:RW].rearrange("p (h r) -> p h r", h=H)[:, :, 1]
                final = small[0:1, RW:2 * RW].rearrange("p (h r) -> p h r", h=H)[:, :, n]
                m = dve.do(lambda e: e.tensor_tensor(scale[:, j % 2, :], old[:], first, ALU.subtract),
                           [st["edge_rows"], z5, scaled.get(j - 2), st.get("old")])
                st["scale", j] = act.do(lambda e: e.activation(scale[:, j % 2, :], scale[:, j % 2, :], ACT.Exp), [m])
                m = dve.do(lambda e: e.tensor_copy(old[:], final), [m])
                st["small"] = st["old"] = dve.do(lambda e: e.tensor_copy(
                    row_f[:, 1:1 + RW].rearrange("p (h r) -> p h r", h=H)[:, :, 0], final), [m, st["fs"]])

        m_mask, m_w = {}, {}

        def weigh(i):
            j, r, u = i // BATCH, i % BATCH + 1, i % sums.RING
            ww = ex[:, j % 2, :, r]
            m_mask[i] = sums.make_masks(i)
            v_read[i] = dve.do(lambda e: e.tensor_tensor(
                sums.vals[:, u, 0:D].rearrange("p (h c) -> p h c", h=H),
                vj[:, i % NV, :].rearrange("p (h c) -> p h c", h=H),
                ww.unsqueeze(2).to_broadcast([P, H, C]), ALU.mult), [ex_ready[j], v_written[i], sums.free(i)])
            m_w[i] = ex_read[j] = act.do(lambda e: e.activation(
                sums.vals[:, u, D:VALS], ww, ACT.Copy), [sums.free(i), v_read[i]])

        rest = {}

        def sum_first(p):
            i, j = 2 * p, 2 * p // BATCH
            both = [m[n] for m in (v_read, m_w, m_mask) for n in (i + 1, i) if n in m]
            if i % BATCH == 0 and i > 0:
                m = scaled[j] = sums.carry(p, [v_read[i], m_w[i], st["scale", j]], scale=scale[:, j % 2, :])
            else:
                m = sums.carry(p, [v_read[i], m_w[i]])
            rest[p] = [*both, m]
            sums.sum_first(p, both)

        def sum_rest(p):
            sums.sum_rest(p, rest[p])
            sums.keep(p - 1)

        for c in range(NE - 1):
            load_attrs(c)
        todo, begin = {}, 0
        for j in range(batches):
            begin = max(min(T, (j + 1) * BATCH), begin + 8)
            for step in range(8):
                todo.setdefault(begin + step, []).append((j, step))
        AHEAD = 5
        for i in range(AHEAD):
            gather(i)
        edge_product(0)
        for i in range(T + LAG + 4):
            if i < T:
                if i % CH == 0 and i // CH + NE - 1 < -(-T // CH):
                    load_attrs(i // CH + NE - 1)
                if i % BATCH == 0:
                    load_runs(i // BATCH)
                if i % BATCH == RUNS_READY or i == T - 1 and i % BATCH < RUNS_READY:
                    penalties(i // BATCH)
                if i + AHEAD < T:
                    gather(i + AHEAD)
                if i + 1 < T:
                    edge_product(i + 1)
                logits(i)
            for j, step in todo.get(i, ()):
                setup_step(j, step)
            if 0 <= i - LAG < T:
                weigh(i - LAG)
            n = i - LAG
            if n >= 2 and n % 2 == 0 and n - 2 < T:
                sum_first((n - 2) // 2)
            if n >= 3 and n % 2 == 1 and n - 3 < T:
                sum_rest((n - 3) // 2)
        sums.keep((T - 1) // 2)
        sums.finish()



class NodeTools:
    def __init__(self, ph, k):
        self.ph, self.k = ph, k
        self.stats = ph.sb("stats", [P, 2, 6])
        self.mv = ph.sb("mv", [P, 2, 2])
        self.rs = ph.sb("rs", [P, 2])
        self.eps = ph.sb("eps", [P, 1])
        self.eps_ok = ph.dve.do(lambda e: e.memset(self.eps[:], LN_EPS))
        self.read = {}

    def layernorm(self, b, out, x, after):
        dve, act, u = self.ph.dve, self.ph.act, b % 2
        m = dve.do(lambda e: e.bn_stats(self.stats[:, u, :], x), [*after, self.read.get(b - 2)])
        m1 = dve.do(lambda e: e.bn_aggr(self.mv[:, u, :], self.stats[:, u, :]), [m])
        m = act.do(lambda e: e.activation(self.rs[:, u:u + 1], self.mv[:, u, 1:2], ACT.Sqrt, bias=self.eps[:, 0:1]),
                   [m1, self.eps_ok])
        m = dve.do(lambda e: e.reciprocal(self.rs[:, u:u + 1], self.rs[:, u:u + 1]), [m])
        self.read[b] = dve.do(lambda e: e.tensor_scalar(
            out, x, self.mv[:, u, 0:1], self.rs[:, u:u + 1], ALU.subtract, ALU.mult), [m, m1])
        return self.read[b]


class Turn:

    def __init__(self, ph, k, name):
        self.ph, self.k = ph, k
        self.psum = ph.psum(f"{name}_turn")
        self.cols = ph.sb(f"{name}_cols", [P, 2, KD, P])
        self.copied, self.used = {}, {}

    def __call__(self, b, x, after):
        ph, u = self.ph, b % 2
        for a in range(KD):
            m = ph.pe.do(lambda e, a=a: e.transpose(
                self.psum[:, a * P:(a + 1) * P], x[:, a * P:(a + 1) * P], self.k["ident"][:]),
                [*after, self.copied.get(b - 1)])
        self.copied[b] = ph.act.do(lambda e: e.activation(
            self.cols[:, u, :, :].rearrange("p a n -> p (a n)"), self.psum[:, 0:KD * P], ACT.Copy),
            [m, self.used.get(b - 2)])
        return self.copied[b]


class Project:

    def __init__(self, ph, k, s, t, conv, turn, tables):
        self.ph, self.turn, self.tables = ph, turn, tables
        self.w = ph.sb("w_proj", [P, KD, 4 * D])
        self.bias = ph.sb("b_proj", [P, 4 * D])
        self.psum = [ph.psum("proj0"), ph.psum("proj1")]
        self.rows = ph.sb("proj_rows", [P, 2, 4 * D])
        self.stores = ph.slots("proj", 2)
        load = ph.slots("proj_w", 1)[0]
        ph.sp.dma(lambda e: e.dma_start(self.w[:], t[f"w_proj{conv}"]), load)
        self.got = ph.sp.dma(lambda e: e.dma_start(self.bias[:], t[f"b_proj{conv}"].to_broadcast([P, 4 * D])), load)
        self.added, self.stored = {}, {}

    def __call__(self, b, cols_ready):
        ph, u = self.ph, b % 2
        kv, qs = self.tables
        for half in range(2):
            cs = slice(half * 2 * D, (half + 1) * 2 * D)
            for a in range(KD):
                m = ph.pe.do(lambda e, a=a, cs=cs, half=half: e.matmul(
                    self.psum[half][:, 0:2 * D], self.turn.cols[:, u, a, :], self.w[:, a, cs],
                    start=(a == 0), stop=(a == KD - 1)), [cols_ready, self.got, self.added.get((b - 1, half))])
            self.turn.used[b] = m
            self.added[b, half] = ph.dve.do(lambda e, cs=cs, half=half: e.tensor_tensor(
                self.rows[:, u, cs], self.psum[half][:, 0:2 * D], self.bias[:, cs], ALU.add),
                [m, self.stored.get(b - 2)])
        r = slice(b * P, (b + 1) * P)
        ph.sp.dma(lambda e: e.dma_start(kv[r, :], self.rows[:, u, 0:2 * D]), self.stores[u], [self.added[b, 0]])
        ph.sp.dma(lambda e: e.dma_start(qs[0][r, :], self.rows[:, u, 2 * D:3 * D]), self.stores[u], [self.added[b, 1]])
        self.stored[b] = ph.sp.dma(lambda e: e.dma_start(qs[1][r, :], self.rows[:, u, 3 * D:4 * D]), self.stores[u])

    def finish(self):
        self.ph.sp.hold([(x.sem, x.count) for x in self.stores])


def gather_sums(ph, k, s, width, table, n=3):
    buf = ph.sb("agg", [P, n, width])
    slots = ph.slots("agg", n)
    marks, read = {}, {}

    def fetch(b):
        if b < s.blocks:
            marks[b] = ph.pool.dma(lambda e: e.indirect_dma_start(
                out=buf[:, b % n, :], out_offset=None, **rows_of(table, k["last_row"][:, b:b + 1])),
                slots[b % n], [read.get(b - n)])

    return buf, marks, read, fetch


def node_pass_resnorm(nc, k, t, s, sums_table, x1_table, tables):
    with Phase(nc, "n0") as ph:
        pe, dve, act, sp = ph.pe, ph.dve, ph.act, ph.sp
        tools = NodeTools(ph, k)
        agg, agg_got, agg_read, fetch = gather_sums(ph, k, s, D, sums_table)
        w12 = ph.sb("w12", [P, 2, KD, D])
        bias = ph.sb("bias", [P, 2, D])
        NX = 4
        x = ph.sb("x", [P, NX, D])
        xt = ph.sb("xt", [P, NX, KD, P])
        y = ph.sb("y", [P, 2, D])
        nb = ph.sb("nb", [P, 2, D])
        o = ph.sb("o", [P, 2, D])
        o2 = ph.sb("o2", [P, 2, D])
        x1 = ph.sb("x1", [P, 3, D])
        ss = ph.sb("ss", [P, 2])
        lin = [ph.psum("lin0"), ph.psum("lin1")]
        turn_y, turn_x = Turn(ph, k, "y"), Turn(ph, k, "x")
        project = Project(ph, k, s, t, 1, turn_x, tables)
        load_w = ph.slots("w", 1)[0]
        sp.dma(lambda e: e.dma_start(w12[:, 0, :, :], t["w1"]), load_w)
        sp.dma(lambda e: e.dma_start(w12[:, 1, :, :], t["w2"]), load_w)
        sp.dma(lambda e: e.dma_start(bias[:, 0, :], t["b1"].to_broadcast([P, D])), load_w)
        m_w = sp.dma(lambda e: e.dma_start(bias[:, 1, :], t["b2"].to_broadcast([P, D])), load_w)
        m_bias = dve.do(lambda e: e.tensor_tensor(bias[:, 0, :], bias[:, 0, :], bias[:, 1, :], ALU.add), [m_w])
        got_x, stores = ph.slots("x", NX), ph.slots("x1", 3)
        x_mark, x_read, lin_read, lin_done, x1_done, x1_stored, o_read = {}, {}, {}, {}, {}, {}, {}

        def load(b):
            if b < s.blocks:
                u = b % NX
                sp.dma(lambda e: e.dma_start(x[:, u, :], t["x_rows"][b * P:(b + 1) * P, :]), got_x[u],
                       [x_read.get(b - NX), lin_done.get(b - NX)])
                x_mark[b] = sp.dma(lambda e: e.dma_start(xt[:, u, :, :], t["x_cols"][:, :, b * P:(b + 1) * P]), got_x[u])
                fetch(b)

        def first(b):
            u, v = b % 2, b % 3
            m = dve.do(lambda e: e.tensor_scalar(nb[:, u, :], agg[:, v, :], k["has_edge"][:, b:b + 1], None, ALU.mult),
                       [agg_got[b]])
            agg_read[b] = m
            m1 = dve.do(lambda e: e.tensor_tensor(y[:, u, :], nb[:, u, :], x[:, b % NX, :], ALU.mult), [m, x_mark[b], turn_y.copied.get(b - 2)])
            m1 = dve.do(lambda e: e.tensor_tensor(y[:, u, :], y[:, u, :], nb[:, u, :], ALU.add), [m1])
            cols = turn_y(b, y[:, u, :], [m1])
            for a in range(KD):
                pe.do(lambda e, a=a: e.matmul(lin[u][:, 0:D], xt[:, b % NX, a, :], w12[:, 0, a, :], start=(a == 0), stop=False),
                      [x_mark[b], m_w, lin_read.get(b - 2)])
            for a in range(KD):
                m = pe.do(lambda e, a=a: e.matmul(lin[u][:, 0:D], turn_y.cols[:, u, a, :], w12[:, 1, a, :],
                                                  start=False, stop=(a == KD - 1)), [cols])
            lin_done[b] = turn_y.used[b] = m

        def second(b):
            u, v = b % 2, b % 3
            m = lin_read[b] = dve.do(lambda e: e.tensor_tensor(o[:, u, :], lin[u][:, 0:D], bias[:, 0, :], ALU.add),
                                     [lin_done[b], m_bias, o_read.get(b - 2)])
            m = dve.do(lambda e: e.scalar_tensor_tensor(
                o2[:, u, :], o[:, u, :], LEAKY, o[:, u, :], ALU.mult, ALU.max), [m, o_read.get(b - 2)])
            q = act.do(lambda e: e.activation(o[:, u, :], o2[:, u, :], ACT.Square, accum_out=ss[:, u:u + 1]), [m])
            q = act.do(lambda e: e.activation(ss[:, u:u + 1], ss[:, u:u + 1], ACT.Sqrt), [q])
            q = dve.do(lambda e: e.tensor_scalar(ss[:, u:u + 1], ss[:, u:u + 1], NORM_EPS, None, ALU.max), [q])
            q = dve.do(lambda e: e.reciprocal(ss[:, u:u + 1], ss[:, u:u + 1]), [q])
            m = x_read[b] = dve.do(lambda e: e.scalar_tensor_tensor(
                o[:, u, :], o2[:, u, :], ss[:, u:u + 1], x[:, b % NX, :], ALU.mult, ALU.add), [q])
            m = x1_done[b] = o_read[b] = tools.layernorm(b, x1[:, v, :], o[:, u, :], [m, x1_stored.get(b - 3), turn_x.copied.get(b - 3)])
            x1_stored[b] = sp.dma(lambda e: e.dma_start(x1_table[b * P:(b + 1) * P, :], x1[:, v, :]), stores[v], [m])

        for b in range(2):
            load(b)
        for b in range(s.blocks + 2):
            load(b + 2)
            if b < s.blocks:
                first(b)
            if 0 <= b - 1 < s.blocks:
                second(b - 1)
            if 0 <= b - 2:
                project(b - 2, turn_x(b - 2, x1[:, (b - 2) % 3, :], [x1_done[b - 2]]))
        project.finish()
        sp.hold([(x.sem, x.count) for x in stores])


def conv_rows(ph, k, s, sums_table, skip_table):
    agg, agg_got, agg_read, fetch = gather_sums(ph, k, s, VALS, sums_table)
    skip = ph.sb("skip", [P, 3, D])
    got = ph.slots("skip", 3)
    rec = ph.sb("rec", [P, 2, H])
    rows = ph.sb("rows", [P, 2, D])
    marks, read, used = {}, {}, {}

    def load(b):
        if b < s.blocks:
            fetch(b)
            marks[b] = ph.sp.dma(lambda e: e.dma_start(skip[:, b % 3, :], skip_table[b * P:(b + 1) * P, :]),
                                 got[b % 3], [read.get(b - 3)])

    def rows_ready(b):
        dve, u, v = ph.dve, b % 2, b % 3
        m = dve.do(lambda e: e.tensor_scalar(rec[:, u, :], agg[:, v, D:VALS], SUM_EPS, None, ALU.add), [agg_got[b]])
        m = dve.do(lambda e: e.reciprocal(rec[:, u, :], rec[:, u, :]), [m])
        m = dve.do(lambda e: e.tensor_scalar(rec[:, u, :], rec[:, u, :], k["has_edge"][:, b:b + 1], None, ALU.mult), [m])
        m = agg_read[b] = dve.do(lambda e: e.tensor_tensor(
            rows[:, u, :].rearrange("p (h c) -> p h c", h=H), agg[:, v, 0:D].rearrange("p (h c) -> p h c", h=H),
            rec[:, u, :].unsqueeze(2).to_broadcast([P, H, C]), ALU.mult), [m, used.get(b - 2)])
        m = read[b] = dve.do(lambda e: e.tensor_tensor(rows[:, u, :], rows[:, u, :], skip[:, v, :], ALU.add), [m, marks[b]])
        return m

    return load, rows, rows_ready, used


def node_pass_hidden(nc, k, t, s, sums_table, skip_table, tables):
    with Phase(nc, "n1") as ph:
        load, rows, rows_ready, used = conv_rows(ph, k, s, sums_table, skip_table)
        turn = Turn(ph, k, "h")
        project = Project(ph, k, s, t, 2, turn, tables)
        done = {}
        for b in range(2):
            load(b)
        for b in range(s.blocks + 1):
            load(b + 2)
            if b < s.blocks:
                m = rows_ready(b)
                done[b] = ph.dve.do(lambda e, b=b: e.tensor_scalar(
                    rows[:, b % 2, :], rows[:, b % 2, :], 0.0, None, ALU.max), [m])
            if b >= 1:
                used[b - 1] = turn(b - 1, rows[:, (b - 1) % 2, :], [done[b - 1]])
                project(b - 1, used[b - 1])
        project.finish()


def node_pass_last(nc, k, t, s, sums_table, skip_table, x1_table, out):
    with Phase(nc, "n2") as ph:
        tools = NodeTools(ph, k)
        load, rows, rows_ready, used = conv_rows(ph, k, s, sums_table, skip_table)
        x1 = ph.sb("x1", [P, 3, D])
        y = ph.sb("y", [P, 2, D])
        got, stores = ph.slots("x1", 3), ph.slots("out", 2)
        marks, read, stored = {}, {}, {}

        def load_all(b):
            load(b)
            if b < s.blocks:
                marks[b] = ph.sp.dma(lambda e: e.dma_start(x1[:, b % 3, :], x1_table[b * P:(b + 1) * P, :]),
                                     got[b % 3], [read.get(b - 3)])

        for b in range(2):
            load_all(b)
        for b in range(s.blocks):
            load_all(b + 2)
            u, n = b % 2, min(P, s.nodes - b * P)
            m = rows_ready(b)
            m = read[b] = ph.dve.do(lambda e, b=b, u=u: e.tensor_tensor(
                rows[:, u, :], rows[:, u, :], x1[:, b % 3, :], ALU.add), [m, marks[b]])
            m = used[b] = tools.layernorm(b, y[:, u, :], rows[:, u, :], [m, stored.get(b - 2)])
            stored[b] = ph.sp.dma(lambda e, b=b, u=u, n=n: e.dma_start(out[b * P:b * P + n, :], y[0:n, u, :]),
                                  stores[u], [m])
        ph.sp.hold([(x.sem, x.count) for x in stores])


def build(nc, t, s, out):
    def scratch(name, shape):
        return nc.dram_tensor(name, shape, F32, kind="Internal").ap()

    slots = s.tiles * P
    sums0 = scratch("sums0", [slots, D])
    sums = [scratch(f"sums{c}", [slots, VALS]) for c in (1, 2)]
    x1 = scratch("x1_rows", [s.rows, D])
    kv = [scratch(f"kv{c}", [s.rows, 2 * D]) for c in (1, 2)]
    q = [scratch(f"q{c}", [s.rows, D]) for c in (1, 2)]
    skip = [scratch(f"skip{c}", [s.rows, D]) for c in (1, 2)]
    with ExitStack() as keep:
        k = constants(nc, keep, t, s)
        singles = single_rows(nc, keep, t, s)
        edge_pass_weighted(nc, k, t, s, sums0)
        node_pass_resnorm(nc, k, t, s, sums0, x1, (kv[0], (q[0], skip[0])))
        edge_pass_attention(nc, "e1", k, t, s, t["w_edge1"], kv[0], q[0], singles, sums[0])
        node_pass_hidden(nc, k, t, s, sums[0], skip[0], (kv[1], (q[1], skip[1])))
        edge_pass_attention(nc, "e2", k, t, s, t["w_edge2"], kv[1], q[1], singles, sums[1])
        node_pass_last(nc, k, t, s, sums[1], skip[1], x1, out)



def lay_out(x, src, dst, edge_attr_194, edge_weight, L0_gnn_W1, L0_gnn_b1, L0_gnn_W2, L0_gnn_b2, **conv):
    n, e, f = x.shape[0], src.shape[0], edge_attr_194.shape[1]
    s = Shapes(n, e, f)

    def slots(a, front, behind):
        line = np.full(s.cols, behind, a.dtype)
        line[0], line[1:1 + e] = front, a
        return np.ascontiguousarray(line[np.arange(s.tiles)[:, None] * OWN + np.arange(P)[None, :]])

    def halves(w, rows):
        full = np.zeros((rows * -(-w.shape[0] // rows), w.shape[1]), w.dtype)
        full[:w.shape[0]] = w
        return np.ascontiguousarray(full.reshape(-1, rows, w.shape[1]).transpose(1, 0, 2))

    dst_rows = slots(dst, s.front, s.behind)
    dst_next = dst_rows.copy()
    dst_next[:, 0] = dst_rows[:, 1]
    x_rows = np.zeros((s.rows, x.shape[1]), x.dtype)
    x_rows[:n] = x
    attr = np.zeros((2 * s.ka, s.cols), edge_attr_194.dtype)
    attr[:f, 1:1 + e] = edge_attr_194.T
    t = {
        "dst_rows": dst_rows,
        "dst_cols": np.ascontiguousarray(dst_rows.T),
        "dst_next_cols": np.ascontiguousarray(dst_next.T),
        "src_cols": np.ascontiguousarray(slots(src, 0, 0).T),
        "weight_cols": np.ascontiguousarray(slots(edge_weight, 0, 0).T),
        "x_rows": x_rows,
        "x_cols": halves(x_rows.T, P),
        "attr_cols": np.ascontiguousarray(attr.reshape(2, s.ka, s.cols).transpose(1, 0, 2)),
        "w1": halves(L0_gnn_W1.T, P), "w2": halves(L0_gnn_W2.T, P),
        "b1": L0_gnn_b1[None, :], "b2": L0_gnn_b2[None, :],
    }
    for c in (1, 2):
        g = lambda name: conv[f"L1_gnn_{name}{c}"]
        t[f"w_proj{c}"] = halves(np.concatenate([g("Wk"), g("Wv"), g("Wq"), g("Ws")], axis=1), P)
        t[f"b_proj{c}"] = np.concatenate([g("bk"), g("bv"), g("bq"), g("bs")])[None, :]
        t[f"w_edge{c}"] = halves(g("We"), s.ka)
    return s, {name: np.ascontiguousarray(a) for name, a in t.items()}


def kernel(**inputs):
    import concourse.bacc as _bacc
    from concourse.bass_utils import run_bass_kernel_spmd as _run

    s, arrays = lay_out(**{name: np.asarray(a) for name, a in inputs.items()})
    nc = _bacc.Bacc("TRN2", target_bir_lowering=False, num_devices=1)
    t = {name: nc.dram_tensor(name, a.shape, mybir.dt.from_np(a.dtype), kind="ExternalInput").ap()
         for name, a in arrays.items()}
    out = nc.dram_tensor("out", (s.nodes, D), F32, kind="ExternalOutput").ap()
    build(nc, t, s, out)
    r = _run(nc, [arrays], core_ids=[0])
    return r.results[0]["out"]
```

```python
from contextlib import ExitStack
from itertools import zip_longest

import numpy as np

import concourse.bass as bass
from concourse import mybir

P = 128
OWN = P - 1
D = 256
H = 4
C = D // H
KD = D // P
BATCH = 16
ROWS = 32
VALS = D + H
BIG = float(2.0 ** 100)
LEAKY = 0.2
NORM_EPS = 1e-12
LN_EPS = 1e-5
SUM_EPS = 1e-16
NODE_AHEAD = 5

F32 = mybir.dt.float32
BF16 = mybir.dt.bfloat16
I32 = mybir.dt.int32
ALU = mybir.AluOpType
ACT = mybir.ActivationFunctionType


class Shapes:
    def __init__(self, nodes, edges, attrs):
        self.nodes, self.edges, self.attrs = nodes, edges, attrs
        self.tiles = -(-edges // OWN)
        self.blocks = -(-nodes // P)
        self.rows = self.blocks * P
        self.cols = self.tiles * OWN + 1
        self.ka = -(-attrs // 32) * 16
        self.front, self.behind = self.rows - 2, self.rows - 1
        assert nodes <= self.rows - 2 and BATCH % 2 == 0 and BATCH < ROWS


class Lane:

    def __init__(self, sem):
        self.sem, self.count, self.program, self.seen = sem, 0, [], {}

    def _add(self, build, after, sem, step):
        waits = []
        for mark in after:
            if mark is not None and self.seen.get(id(mark[0]), 0) < mark[1]:
                self.seen[id(mark[0])] = mark[1]
                waits.append(mark)
        self.program.append((waits, build, sem, step))

    def do(self, build, after=()):
        self._add(build, after, self.sem, 1)
        self.count += 1
        return self.sem, self.count

    def dma(self, build, slot, after=()):
        self._add(build, after, slot.sem, 16)
        slot.count += 16
        return slot.sem, slot.count

    def hold(self, after):
        self._add(None, after, None, 0)

    def play(self, eng):
        for waits, build, sem, step in self.program:
            for s, value in waits:
                eng.wait_ge(s, value)
            if build is not None:
                build(eng).then_inc(sem, step)


class Slot:
    def __init__(self, sem):
        self.sem, self.count = sem, 0


class Phase:

    def __init__(self, nc, name):
        self.nc, self.name, self.stack = nc, name, ExitStack()

    def __enter__(self):
        self.stack.__enter__()
        self.pe, self.dve, self.act, self.pool = (Lane(self.sem(n)) for n in ("pe", "dve", "act", "pool"))
        self.sp = Lane(None)
        return self

    def sb(self, name, shape, dtype=F32):
        return self.stack.enter_context(self.nc.sbuf_tensor(f"{self.name}_{name}", shape, dtype))

    def psum(self, name):
        return self.stack.enter_context(self.nc.psum_tensor(f"{self.name}_{name}", [P, 512], F32))

    def sem(self, name):
        return self.stack.enter_context(self.nc.semaphore(f"{self.name}_{name}_done"))

    def slots(self, name, n):
        return [Slot(self.sem(f"{name}{i}")) for i in range(n)]

    def __exit__(self, kind, *rest):
        if kind is None:
            with self.nc.Block() as block:
                for start, lane in ((block.tensor, self.pe), (block.vector, self.dve), (block.scalar, self.act),
                                    (block.gpsimd, self.pool), (block.sync, self.sp)):
                    start(lane.play)
        return self.stack.__exit__(kind, *rest)


def rows_of(table, index):
    return dict(in_=table, in_offset=bass.IndirectOffsetOnAxis(ap=index, axis=0))



def constants(nc, keep, t, s):
    k = {}

    def sb(name, shape, dtype=F32):
        k[name] = keep.enter_context(nc.sbuf_tensor(name, shape, dtype))
        return k[name]

    ident = sb("ident", [P, P])
    slot_of = sb("slot_of", [P, P])
    upto = sb("upto", [P, P])
    upto_open = sb("upto_open", [P, P])
    run_end = sb("run_end", [P, s.tiles])
    link_end = sb("link_end", [P, s.tiles])
    src = sb("src_sb", [P, s.tiles], I32)
    dst = sb("dst_sb", [P, s.tiles], I32)
    weight = sb("weight_sb", [P, s.tiles])
    sb("last_row", [P, s.blocks], I32)
    sb("has_edge", [P, s.blocks])
    k["singles"] = keep.enter_context(nc.sbuf_tensor("singles", [1, -(-s.tiles // BATCH), H * ROWS + 1], F32))

    groups = -(-s.tiles // P)
    with Phase(nc, "setup") as ph:
        pe, dve, pool, sp = ph.pe, ph.dve, ph.pool, ph.sp
        load = ph.slots("load", 5)
        got_src = sp.dma(lambda e: e.dma_start(src[:], t["src_cols"]), load[0])
        got_dst = sp.dma(lambda e: e.dma_start(dst[:], t["dst_cols"]), load[0])
        got_w = sp.dma(lambda e: e.dma_start(weight[:], t["weight_cols"]), load[0])

        z = pool.do(lambda e: e.memset(ident[:], 0.0))
        m_id = pool.do(lambda e: e.affine_select(
            out=ident[:], in_=ident[:], compare_op=ALU.not_equal, fill=1.0, base=0,
            pattern=[[-1, P]], channel_multiplier=1), [z])
        iota = ph.sb("iota", [P, P])
        m_io = pool.do(lambda e: e.iota(iota[:], pattern=[[1, P]], base=0, channel_multiplier=0,
                                        allow_small_or_imprecise_dtypes=True))
        a = pool.do(lambda e: e.iota(slot_of[:], pattern=[[1, P]], base=0, channel_multiplier=0,
                                     allow_small_or_imprecise_dtypes=True))
        a = pool.do(lambda e: e.memset(slot_of[:, 0:1], float(P - 1)), [a])
        b = pool.do(lambda e: e.memset(upto[:], 1.0))
        b = pool.do(lambda e: e.affine_select(
            out=upto[:], in_=upto[:], compare_op=ALU.is_ge, fill=0.0, base=0,
            pattern=[[1, P]], channel_multiplier=-1), [b])
        b = pool.do(lambda e: e.memset(upto[:, 0:1], 1.0), [b])

        c = pool.do(lambda e: e.memset(upto_open[:], 1.0))
        c = pool.do(lambda e: e.affine_select(
            out=upto_open[:], in_=upto_open[:], compare_op=ALU.is_ge, fill=0.0, base=0,
            pattern=[[1, P]], channel_multiplier=-1), [c])
        c = pool.do(lambda e: e.memset(upto_open[:, 0:1], 1.0), [c])
        c = pool.do(lambda e: e.memset(upto_open[0:1, :], 0.0), [c])

        d_int = [ph.sb(f"d_int{i}", [P, P], I32) for i in range(2)]
        d_f = [ph.sb(f"d_f{i}", [P, P]) for i in range(2)]
        same = [ph.sb(f"same{i}", [P, P]) for i in range(2)]
        ends = [ph.sb(f"ends{i}", [P, P]) for i in range(2)]
        turned = ph.psum("turned")
        zero = [dve.do(lambda e, x=x: e.memset(x[:], 0.0)) for x in same + ends]
        same_m = zero[:2]
        copied = [None, None]
        pe_read = [zero[2], zero[3]]
        for g in range(groups):
            n, u = min(P, s.tiles - g * P), g % 2
            m = sp.dma(lambda e, g=g, n=n, u=u: e.dma_start(d_int[u][0:n, :], t["dst_rows"][g * P:g * P + n, :]),
                       load[1 + u], [copied[u]])
            m = copied[u] = dve.do(lambda e, n=n, u=u: e.tensor_copy(d_f[u][0:n, :], d_int[u][0:n, :]), [m, same_m[u]])
            m = same_m[u] = dve.do(lambda e, n=n, u=u: e.tensor_tensor(
                same[u][0:n, 0:P - 1], d_f[u][0:n, 1:P], d_f[u][0:n, 0:P - 1], ALU.is_equal), [m, same_m[u]])
            m = dve.do(lambda e, n=n, u=u: e.tensor_tensor_scan(
                ends[u][0:n, ::-1], same[u][0:n, ::-1], iota[0:n, ::-1], 0.0, ALU.mult, ALU.max),
                [m, m_io, pe_read[u]])
            m = pe_read[u] = pe.do(lambda e, n=n, u=u: e.transpose(
                turned[:, u * P:u * P + n], ends[u][0:n, :], ident[0:n, 0:n]), [m, m_id])
            dve.do(lambda e, g=g, n=n, u=u: e.tensor_copy(
                run_end[:, g * P:g * P + n], turned[:, u * P:u * P + n]), [m])
            pe_read[u] = (dve.sem, dve.count)
        goes_on = ph.sb("goes_on", [P, s.tiles])
        spread = ph.psum("spread")
        ends_ready = (dve.sem, dve.count)
        z = dve.do(lambda e: e.memset(link_end[:], -1.0))
        m1 = dve.do(lambda e: e.tensor_scalar(goes_on[:], run_end[:], float(P - 1), None, ALU.is_equal), [ends_ready])
        m = None
        for a in range(1, s.tiles, 512):
            n = min(512, s.tiles - a)
            m = pe.do(lambda e, a=a, n=n: e.matmul(spread[:, 0:n], upto[0:1, :], run_end[0:1, a:a + n],
                                                   start=True, stop=True), [ends_ready, b, m])
            m = dve.do(lambda e, a=a, n=n: e.scalar_tensor_tensor(
                link_end[:, a:a + n], spread[:, 0:n], 1.0, goes_on[:, a - 1:a - 1 + n], ALU.add, ALU.mult), [m, z, m1])
        dve.do(lambda e: e.tensor_scalar(link_end[:, 1:], link_end[:, 1:], -1.0, None, ALU.add), [m])
        pool.do(lambda e: e.memset(k["singles"][:], -BIG))
        sp.hold([got_src, got_dst, got_w])
    return k



class RunSums:

    GROUP = 4
    PAIRS = 3
    RING = 2 * PAIRS

    def __init__(self, ph, k, s, width, table):
        self.ph, self.k, self.s, self.width, self.table = ph, k, s, width, table
        self.mask = ph.sb("run_mask", [P, self.RING, P])
        self.link = ph.sb("link_mask", [P, self.PAIRS, P])
        self.vals = ph.sb("vals", [P, self.RING, width])
        self.out = [[ph.psum(f"sum{u}{half}") for half in range(2)] for u in range(2)]
        self.rows = ph.sb("sum_rows", [P, 2, self.GROUP, width])
        self.stores = ph.slots("store", 2)
        self.summed = {}
        self.used = {}
        self.evac, self.stored = {}, {}
        self.view = table.rearrange("(t p) c -> p t c", p=P)

    def free(self, i):
        return self.used.get(i // 2 - self.PAIRS)

    def make_masks(self, i):
        k, u, dve = self.k, i % self.RING, self.ph.dve
        upto = k["upto"] if i % 2 == 0 else k["upto_open"]
        m = dve.do(lambda e: e.scalar_tensor_tensor(
            self.mask[:, u, :], k["slot_of"][:], k["run_end"][:, i:i + 1], upto[:], ALU.is_le, ALU.mult),
            [self.free(i)])
        if i % 2 == 0:
            return m
        return dve.do(lambda e: e.tensor_scalar(
            self.link[:, i // 2 % self.PAIRS, :], k["slot_of"][:], k["link_end"][:, i:i + 1], None, ALU.is_le))

    def carry(self, p, after, scale=None):
        act, dve, v = self.ph.act, self.ph.dve, self.vals
        w, u = self.width, 2 * p % self.RING
        if p == 0:
            return dve.do(lambda e: e.memset(v[0:1, u, :], 0.0), after)
        prev = self.out[(p - 1) % 2][1]
        m = act.do(lambda e: e.activation(v[0:1, u, :], prev[0:1, 0:w], ACT.Copy), after + [self.summed[2 * p - 1]])
        if scale is None:
            return m
        row = v[0:1, u, 0:D].rearrange("p (h c) -> p h c", h=H)
        m = dve.do(lambda e: e.tensor_tensor(row, row, scale.unsqueeze(2).to_broadcast([1, H, C]), ALU.mult), [m])
        return dve.do(lambda e: e.tensor_tensor(v[0:1, u, D:w], v[0:1, u, D:w], scale, ALU.mult), [m])

    def sum_first(self, p, after):
        i, out, w, u = 2 * p + 1, self.out[p % 2][1], self.width, (2 * p + 1) % self.RING
        if i < self.s.tiles:
            self.ph.pe.do(lambda e: e.matmul(
                out[:, 0:w], self.mask[:, u, :], self.vals[:, u, :], start=True, stop=False),
                after + [self.evac.get(i - 4)])

    def sum_rest(self, p, after):
        pe, w, u = self.ph.pe, self.width, 2 * p % self.RING
        first, second = self.out[p % 2]
        if 2 * p + 1 < self.s.tiles:
            self.summed[2 * p + 1] = pe.do(lambda e: e.matmul(
                second[:, 0:w], self.link[:, p % self.PAIRS, :], self.vals[:, u, :], start=False, stop=True), after)
        self.summed[2 * p] = self.used[p] = pe.do(lambda e: e.matmul(
            first[:, 0:w], self.mask[:, u, :], self.vals[:, u, :], start=True, stop=True),
            after + [self.evac.get(2 * p - 4)])

    def keep(self, p):
        if p < 0:
            return
        ph, w, grp, end = self.ph, self.width, self.GROUP, min(2 * p + 2, self.s.tiles)
        g = 2 * p // grp
        for i in range(end - 1, 2 * p - 1, -1):
            out = self.out[p % 2][i % 2]
            self.evac[i] = ph.act.do(lambda e, i=i, out=out: e.activation(
                self.rows[:, g % 2, i % grp, :], out[:, 0:w], ACT.Copy), [self.summed[i], self.stored.get(g - 2)])
        if end % grp == 0 or end == self.s.tiles:
            self.stored[g] = ph.sp.dma(lambda e: e.dma_start(
                self.view[:, g * grp:end, :], self.rows[:, g % 2, 0:end - g * grp, :]),
                self.stores[g % 2], [self.evac[2 * p]])

    def finish(self):
        self.ph.sp.hold([(x.sem, x.count) for x in self.stores])


def single_rows(ph, k, t, s):
    dve, sp, singles = ph.dve, ph.sp, k["singles"]
    ends = ph.sb("tile_ends", [1, 2, s.tiles], I32)
    endf = ph.sb("tile_endf", [1, 2, s.tiles])
    pen = ph.sb("tile_pen", [1, s.tiles])
    load = ph.slots("tile_ends", 1)[0]
    sp.dma(lambda e: e.dma_start(ends[:, 0, :], t["dst_cols"][0:1, :]), load)
    m = sp.dma(lambda e: e.dma_start(ends[:, 1, :], t["dst_cols"][P - 1:P, :]), load)
    yield
    m = dve.do(lambda e: e.tensor_copy(endf[:], ends[:]), [m])
    yield
    m = dve.do(lambda e: e.tensor_tensor(pen[:], endf[:, 0, :], endf[:, 1, :], ALU.not_equal), [m])
    yield
    m = dve.do(lambda e: e.tensor_scalar(pen[:], pen[:], -BIG, None, ALU.mult), [m])
    full, left = divmod(s.tiles, BATCH)
    for h in range(H):
        at = ROWS * h + 1
        yield
        if full:
            dve.do(lambda e, at=at: e.tensor_copy(
                singles[:, 0:full, at:at + BATCH],
                pen[:, 0:full * BATCH].rearrange("p (j n) -> p j n", n=BATCH)), [m])
        if left:
            dve.do(lambda e, at=at: e.tensor_copy(singles[:, full, at:at + left], pen[:, full * BATCH:]), [m])


class BlockProduct:

    def __init__(self, ph, s, cols, w, biases, table, psum):
        self.ph, self.s, self.cols_table, self.table, self.psum = ph, s, cols, table, psum
        self.cols = ph.sb("block_cols", [P, 2, KD, P])
        self.w = ph.sb("block_w", [P, KD, D])
        self.bias = ph.sb("block_bias", [P, len(biases), D])
        self.rows = ph.sb("block_rows", [P, 2, D])
        self.loads, self.stores = ph.slots("block_cols", 2), ph.slots("block_rows", 2)
        slot = ph.slots("block_w", 1)[0]
        self.got_w = ph.sp.dma(lambda e: e.dma_start(self.w[:], w), slot)
        for n, bias in enumerate(biases):
            self.got_w = ph.sp.dma(lambda e, n=n, bias=bias: e.dma_start(
                self.bias[:, n, :], bias.to_broadcast([P, D])), slot)
        self.got_bias = self.got_w
        for n in range(1, len(biases)):
            self.got_bias = ph.dve.do(lambda e, n=n: e.tensor_tensor(
                self.bias[:, 0, :], self.bias[:, 0, :], self.bias[:, n, :], ALU.add), [self.got_bias])
        self.got, self.product, self.added, self.stored = {}, {}, {}, {}
        self.load(0)

    def load(self, b):
        if b < self.s.blocks:
            self.got[b] = self.ph.sp.dma(lambda e: e.dma_start(
                self.cols[:, b % 2, :, :], self.cols_table[:, :, b * P:(b + 1) * P]),
                self.loads[b % 2], [self.product.get(b - 2)])

    def begin(self, i, after=()):
        n, tiles = self.s.blocks, self.s.tiles
        self.due = range(i * n // tiles, (i + 1) * n // tiles)
        if self.due:
            self.multiply(self.due[0], after)

    def end(self):
        for b in self.due:
            if b > self.due[0]:
                self.multiply(b)
            self.add(b)
        return self.added[self.due[-1]] if self.due else None

    def multiply(self, b, after=()):
        self.load(b + 1)
        for a in range(KD):
            m = self.ph.pe.do(lambda e, a=a: e.matmul(
                self.psum, self.cols[:, b % 2, a, :], self.w[:, a, :], start=(a == 0), stop=(a == KD - 1)),
                [self.got[b], self.got_w, self.added.get(b - 1), *after])
        self.product[b] = m

    def add(self, b):
        self.added[b] = self.ph.dve.do(lambda e: e.tensor_tensor(
            self.rows[:, b % 2, :], self.psum, self.bias[:, 0, :], ALU.add),
            [self.product[b], self.got_bias, self.stored.get(b - 2)])
        self.stored[b] = self.ph.sp.dma(lambda e: e.dma_start(
            self.table[b * P:(b + 1) * P, :], self.rows[:, b % 2, :]), self.stores[b % 2], [self.added[b]])

    def finish(self):
        self.ph.sp.hold([(x.sem, x.count) for x in self.stores])


def edge_pass_weighted(nc, k, t, s, table, own_table):
    with Phase(nc, "e0") as ph:
        pe, dve, act, pool, sp = ph.pe, ph.dve, ph.act, ph.pool, ph.sp
        AHEAD = 6
        x = ph.sb("x", [P, AHEAD, D])
        got = ph.slots("x", AHEAD)
        sums = RunSums(ph, k, s, D, table)
        own = BlockProduct(ph, s, t["x_cols"], t["w1"], [t["b1"], t["b2"]], own_table, ph.psum("own")[:, 0:D])
        ident = k["ident"]

        load = ph.slots("load", 1)[0]
        num = ph.sb("num", [P, s.tiles], I32)
        part = ph.sb("part", [P, s.tiles], I32)
        hi = ph.sb("hi", [P, s.tiles])
        lo = ph.sb("lo", [P, s.tiles])
        iota = ph.sb("iota", [P, P], BF16)
        one_hi = ph.sb("one_hi", [P, 4, s.blocks], BF16)
        one_lo = ph.sb("one_lo", [P, 4, P], BF16)
        count = ph.psum("count")
        m = sp.dma(lambda e: e.dma_start(num[:], t["dst_next_cols"]), load)
        m1 = dve.do(lambda e: e.tensor_scalar(part[:], num[:], P.bit_length() - 1, None, ALU.arith_shift_right), [m])
        m_hi = dve.do(lambda e: e.tensor_copy(hi[:], part[:]), [m1])
        m2 = dve.do(lambda e: e.tensor_scalar(part[:], num[:], P - 1, None, ALU.bitwise_and), [m_hi])
        m_lo = dve.do(lambda e: e.tensor_copy(lo[:], part[:]), [m2])
        m_io = pool.do(lambda e: e.iota(iota[:], pattern=[[1, P]], base=0, channel_multiplier=0,
                                        allow_small_or_imprecise_dtypes=True))
        counted = {}
        weighted, carried, mask, hot = {}, {}, {}, {}
        R = sums.RING
        singles = single_rows(ph, k, t, s)
        for i in range(s.tiles + 4):
            if i < s.tiles:
                if i % 8 == 0:
                    next(singles, None)
                u = i % AHEAD
                m_x = pool.dma(lambda e, i=i, u=u: e.indirect_dma_start(
                    out=x[:, u, :], out_offset=None, **rows_of(t["x_rows"], k["src_sb"][:, i:i + 1])),
                    got[u], [weighted.get(i - AHEAD)])
                mask[i] = sums.make_masks(i)
                m = dve.do(lambda e, i=i: e.tensor_scalar(one_lo[:, i % 4, :], iota[:], lo[:, i:i + 1], None, ALU.is_equal),
                           [m_lo, m_io, counted.get(i - 4)])
                hot[i] = dve.do(lambda e, i=i: e.tensor_scalar(one_hi[:, i % 4, :], iota[:, 0:s.blocks], hi[:, i:i + 1],
                                                               None, ALU.is_equal), [m_hi, counted.get(i - 4)])
                own.begin(i)
            p = (i - 3) // 2
            if i >= 3 and i % 2 == 1 and 2 * p < s.tiles:
                if p:
                    carried[p] = sums.carry(p, [weighted[2 * p]])
            if i < s.tiles:
                weighted[i] = act.do(lambda e, i=i, u=u: e.activation(
                    sums.vals[:, i % R, :], x[:, u, :], ACT.Copy, scale=k["weight_sb"][:, i:i + 1]), [m_x, sums.free(i)])
            if i >= 3 and i % 2 == 1 and 2 * p < s.tiles:
                if not p:
                    carried[p] = sums.carry(p, [weighted[0]])
                rest = [weighted.get(2 * p + 1), mask.get(2 * p + 1), mask[2 * p], carried[p]]
                sums.sum_first(p, rest[:2])
                sums.sum_rest(p, rest)
                for n in range(2 * p, min(2 * p + 2, s.tiles)):
                    counted[n] = pe.do(lambda e, n=n: e.matmul(
                        count[0:s.blocks, 0:P], one_hi[:, n % 4, :], one_lo[:, n % 4, :],
                        start=(n == 0), stop=(n == s.tiles - 1)), [hot[n]])
                sums.keep(p - 1)
            if i < s.tiles:
                own.end()
        for _ in singles:
            pass
        sums.keep((s.tiles - 1) // 2)
        sums.finish()
        own.finish()

        B = s.blocks
        cnt = ph.sb("cnt", [B, P])
        run = ph.sb("run", [B, P])
        before = ph.sb("before", [B, B])
        has = ph.sb("has", [B, P])
        base = ph.sb("base", [B, 1])
        small = ph.psum("small")
        m_b = pool.do(lambda e: e.memset(before[:], 1.0))
        m_b = pool.do(lambda e: e.affine_select(
            out=before[:], in_=before[:], compare_op=ALU.is_ge, fill=0.0, base=-1,
            pattern=[[1, B]], channel_multiplier=-1), [m_b])
        m = dve.do(lambda e: e.tensor_copy(cnt[:], count[0:B, 0:P]), [counted[s.tiles - 1]])
        m_has = dve.do(lambda e: e.tensor_scalar(has[:], cnt[:], 0.0, None, ALU.is_gt), [m])
        m = dve.do(lambda e: e.tensor_tensor_scan(run[:], cnt[:], cnt[:], 0.0, ALU.add, ALU.bypass), [m])
        m2 = pe.do(lambda e: e.matmul(small[0:B, 0:1], before[:], run[:, P - 1:P], start=True, stop=True), [m, m_b])
        m2 = dve.do(lambda e: e.tensor_copy(base[:], small[0:B, 0:1]), [m2])
        m = dve.do(lambda e: e.tensor_scalar(run[:], run[:], base[:, 0:1], -1.0, ALU.add, ALU.add), [m, m2])
        m = dve.do(lambda e: e.tensor_scalar(run[:], run[:], 0.0, None, ALU.max), [m])
        m = pe.do(lambda e: e.transpose(small[:, 128:128 + B], run[:], ident[0:B, 0:B]), [m, m2])
        m_has = pe.do(lambda e: e.transpose(small[:, 256:256 + B], has[:], ident[0:B, 0:B]), [m_has])
        dve.do(lambda e: e.tensor_copy(k["last_row"][:], small[:, 128:128 + B]), [m_has])
        dve.do(lambda e: e.tensor_copy(k["has_edge"][:], small[:, 256:256 + B]), [m_has])


def edge_pass_attention(nc, name, k, t, s, w_edge, kv_rows, q_rows, table, skip_of):
    CH = 8
    RUNS_READY = 8
    STEPS = 9
    LAG = BATCH + STEPS
    NV, NG, NE = LAG + 4, 9, 3
    ident, singles = k["ident"], k["singles"]
    batches = -(-s.tiles // BATCH)
    T = s.tiles
    with Phase(nc, name) as ph:
        pe, dve, act, pool, sp = ph.pe, ph.dve, ph.act, ph.pool, ph.sp
        sums = RunSums(ph, k, s, VALS, table)
        we = ph.sb("we", [s.ka, 2, D])
        ea = ph.sb("ea", [s.ka, NE, 2, CH * OWN + 1])
        kv = ph.sb("kv", [P, NG, 2, D])
        q = ph.sb("q", [P, NG, D])
        kj = ph.sb("kj", [P, 2, D])
        vj = ph.sb("vj", [P, NV, D])
        logit = ph.sb("logit", [P, 2, H, ROWS])
        ex = ph.sb("ex", [P, 2, H, ROWS])
        pe_e = [ph.psum("e0"), ph.psum("e1")]
        back, small = ph.psum("back"), ph.psum("small")
        cols, w_skip, b_skip, skip_table = skip_of
        skip = BlockProduct(ph, s, cols, w_skip, [b_skip], skip_table, back[:, 2 * P:2 * P + D])
        flat = small[:, 2 * H * ROWS:2 * H * ROWS + P]
        d_int = ph.sb("d_int", [P, 2, P], I32)
        d_f = ph.sb("d_f", [P, P])
        pen = ph.sb("pen", [P, 2, P + 1])
        lr = ph.sb("lr", [P, 2, P])
        fw = ph.sb("fw", [P, P])
        mx = ph.sb("mx", [P, P])
        ends = ph.sb("ends", [P, 2])
        RW = H * ROWS
        row_f = ph.sb("row_f", [1, RW + 2])
        row_b = ph.sb("row_b", [1, RW + 2])
        out_f = ph.sb("out_f", [1, RW + 2])
        out_b = ph.sb("out_b", [1, RW + 2])
        old = ph.sb("old", [1, H])
        scale = ph.sb("scale", [1, 2, H])
        got_rows, got_ea, got_d = (ph.slots(n, c) for n, c in (("rows", NG), ("ea", NE), ("d", 2)))
        w_slot = ph.slots("w", 1)[0]

        got_w = sp.dma(lambda e: e.dma_start(we[:], w_edge), w_slot)
        z0 = dve.do(lambda e: e.memset(logit[:], 0.0))
        z1 = dve.do(lambda e: e.memset(pen[:], 0.0))
        z2 = dve.do(lambda e: e.memset(row_f[:], -BIG))
        z3 = dve.do(lambda e: e.memset(out_f[:], -BIG))
        z4 = dve.do(lambda e: e.memset(out_b[:], -BIG))
        z5 = dve.do(lambda e: e.memset(old[:], -BIG))

        ea_mark, ea_read = {}, {}
        kj_read, v_written, v_read, dots = {}, {}, {}, {}
        turned, ex_ready, scaled = {}, {}, {}
        st = {}
        pen_read, lr_read, ex_read = {}, {}, {}

        def load_attrs(c):
            n = min(CH, T - c * CH) * OWN + 1
            ea_mark[c] = sp.dma(lambda e: e.dma_start(
                ea[:, c % NE, :, 0:n], t["attr_cols"][:, :, c * CH * OWN:c * CH * OWN + n]),
                got_ea[c % NE], [ea_read.get(c - NE)])

        def gather(i):
            u = i % NG
            pool.dma(lambda e: e.indirect_dma_start(
                out=kv[:, u, :, :].rearrange("p a d -> p (a d)"), out_offset=None,
                **rows_of(kv_rows, k["src_sb"][:, i:i + 1])), got_rows[u], [v_written.get(i - NG), dots.get(i - NG)])
            gathered[i] = pool.dma(lambda e: e.indirect_dma_start(
                out=q[:, u, :], out_offset=None, **rows_of(q_rows, k["dst_sb"][:, i:i + 1])), got_rows[u])

        edge_done, gathered = {}, {}

        def edge_product(i):
            c, off = i // CH, (i % CH) * OWN
            for a in range(2):
                m = pe.do(lambda e, a=a: e.matmul(
                    pe_e[i % 2][:, 0:D], ea[:, c % NE, a, off:off + P], we[:, a, :], start=(a == 0), stop=(a == 1)),
                    [ea_mark[c], got_w, v_written.get(i - 2), kj_read.get(i - 2)])
            ea_read[c] = edge_done[i] = m

        def logits(i):
            m, j, r = edge_done[i], i // BATCH, i % BATCH + 1
            mk = kj_read[i] = dve.do(lambda e: e.tensor_tensor(
                kj[:, i % 2, :], kv[:, i % NG, 0, :], pe_e[i % 2][:, 0:D], ALU.add), [gathered[i], m, dots.get(i - 2)])
            v_written[i] = dve.do(lambda e: e.tensor_tensor(
                vj[:, i % NV, :], kv[:, i % NG, 1, :], pe_e[i % 2][:, 0:D], ALU.add), [v_read.get(i - NV)])
            for h in range(H):
                hs = slice(h * C, h * C + C)
                m = dve.do(lambda e, h=h, hs=hs: e.tensor_tensor_reduce(
                    kj[:, i % 2, hs], kj[:, i % 2, hs], q[:, i % NG, hs], 1.0, 0.0, ALU.mult, ALU.add,
                    logit[:, j % 2, h, r:r + 1]), [mk, z0, turned.get(j - 2)])
            dots[i] = m

        def load_runs(j):
            n = min(BATCH, T - j * BATCH)
            for h in range(H):
                m = sp.dma(lambda e, h=h: e.dma_start(
                    d_int[ROWS * h + 1:ROWS * h + 1 + n, j % 2, :], t["dst_rows"][j * BATCH:j * BATCH + n, :]),
                    got_d[j % 2], [st.get(("d", j - 2)), st["dz"]])
            st["runs", j] = m

        def penalties(j):
            m = st["runs", j]
            m = st["d", j] = dve.do(lambda e: e.tensor_copy(d_f[:], d_int[:, j % 2, :]), [m, st.get(("ne", j - 1))])
            m = st["ne", j] = dve.do(lambda e: e.tensor_tensor(
                pen[:, j % 2, 1:P], d_f[:, 1:P], d_f[:, 0:P - 1], ALU.not_equal), [m, z1, pen_read.get(j - 2)])
            st["pen", j] = dve.do(lambda e: e.tensor_scalar(
                pen[:, j % 2, 1:P], pen[:, j % 2, 1:P], -BIG, None, ALU.mult), [m])

        st["dz"] = dve.do(lambda e: e.memset(d_int[:], 0))

        def forward(out, data, j, initial, after):
            return dve.do(lambda e: e.tensor_tensor_scan(
                out[:], pen[:, j % 2, 0:P], data, initial, ALU.add, ALU.max), after)

        def backward(out, data, j, initial, after):
            return dve.do(lambda e: e.tensor_tensor_scan(
                out[:, ::-1], pen[:, j % 2, 1:P + 1][:, ::-1], data[:, ::-1], initial, ALU.add, ALU.max), after)

        def setup_step(j, step):
            n = min(BATCH, T - j * BATCH)
            last = j * BATCH + n - 1
            lrj = lr[:, j % 2, :]
            if step == 0:
                m = turned[j] = pe.do(lambda e: e.transpose(
                    flat, logit[:, j % 2, :, :].rearrange("p h r -> p (h r)"), ident[:]),
                    [dots[last], st.get("lr"), st.get("small")])
                st["lr"] = act.do(lambda e: e.activation(
                    lrj, flat, ACT.Copy, scale=1.0 / float(np.sqrt(C))), [m, lr_read.get(j - 2)])
            elif step == 1:
                m = forward(fw, lrj, j, -BIG, [st["lr"], st["pen", j], st.get("mx")])
                st["mx0"] = backward(mx, fw[:], j, -BIG, [m, st.get("exd"), st.get("edge_rows")])
            elif step == 2:
                m = pe.do(lambda e: e.transpose(small[0:1, 0:RW], mx[:, P - 1:P], ident[:]), [st["mx0"], st.get("small")])
                st["firsts"] = pe.do(lambda e: e.transpose(small[0:1, RW:2 * RW], mx[:, 0:1], ident[:]), [m])
            elif step == 3:
                both = []
                z = [z2, dve.do(lambda e: e.memset(row_b[:], -BIG), [st.get("outs")])]
                for row, at in ((row_f, 0), (row_b, RW)):
                    both.append(dve.do(lambda e, row=row, at=at: e.tensor_copy(
                        row[:, 1:1 + RW].rearrange("p (h r) -> p h r", h=H)[:, :, 1:1 + n],
                        small[0:1, at:at + RW].rearrange("p (h r) -> p h r", h=H)[:, :, 1:1 + n]),
                        [st["firsts"], st.get("outs"), st.get("old"), *z]))
                both.append(dve.do(lambda e: e.tensor_tensor_scan(
                    out_f[:, 1:1 + RW], singles[:, j, 0:RW], row_f[:, 1:1 + RW], -BIG, ALU.add, ALU.max),
                    [*both, z3, st.get("across")]))
                st["outs"] = dve.do(lambda e: e.tensor_tensor_scan(
                    out_b[:, 1:2 + RW][:, ::-1], singles[:, j, :][:, ::-1], row_b[:, 1:2 + RW][:, ::-1], -BIG,
                    ALU.add, ALU.max), [*both, z4])
                st["fs"] = both[-1]
            elif step == 4:
                m = pe.do(lambda e: e.transpose(back[:, P:P + 1], out_f[0:1, 0:RW], ident[0:1, 0:1]),
                          [st["outs"], st["fs"], st.get("ends"), st.get("exc"), st.get("skip")])
                st["across"] = pe.do(lambda e: e.transpose(back[:, P + 1:P + 2], out_b[0:1, 2:2 + RW], ident[0:1, 0:1]), [m])
            elif step == 5:
                st["ends"] = dve.do(lambda e: e.tensor_copy(ends[:], back[:, P:P + 2]), [st["across"], st.get("mx")])
                m = forward(fw, lrj, j, ends[:, 0:1], [st["ends"], st["mx0"]])
                st["mx"] = pen_read[j] = backward(mx, fw[:], j, ends[:, 1:2], [m, st["firsts"]])
            elif step == 6:
                m = st["exd"] = lr_read[j] = dve.do(
                    lambda e: e.tensor_tensor(lrj, lrj, mx[:], ALU.subtract), [st["mx"]])
                lr_read[j] = st["exp"] = act.do(lambda e: e.activation(lrj, lrj, ACT.Exp), [m])
                m = pe.do(lambda e: e.transpose(small[0:1, 0:RW], mx[:, 0:1], ident[:]), [st["mx"], *[st["outs"]]])
                st["edge_rows"] = pe.do(lambda e: e.transpose(small[0:1, RW:2 * RW], mx[:, P - 1:P], ident[:]), [m])
            elif step == 7:
                m = pe.do(lambda e: e.transpose(back[:, 0:P], lrj, ident[:]), [st["exp"], st.get("exc"), st["ends"], st.get("skip")])
                lr_read[j] = m
                st["exc"] = ex_ready[j] = act.do(lambda e: e.activation(
                    ex[:, j % 2, :, :].rearrange("p h r -> p (h r)"), back[:, 0:P], ACT.Copy), [m, ex_read.get(j - 2)])
                first = small[0:1, 0:RW].rearrange("p (h r) -> p h r", h=H)[:, :, 1]
                final = small[0:1, RW:2 * RW].rearrange("p (h r) -> p h r", h=H)[:, :, n]
                m = dve.do(lambda e: e.tensor_tensor(scale[:, j % 2, :], old[:], first, ALU.subtract),
                           [st["edge_rows"], z5, scaled.get(j - 2), st.get("old")])
                st["scale", j] = act.do(lambda e: e.activation(scale[:, j % 2, :], scale[:, j % 2, :], ACT.Exp), [m])
                m = dve.do(lambda e: e.tensor_copy(old[:], final), [m])
                st["small"] = st["old"] = dve.do(lambda e: e.tensor_copy(
                    row_f[:, 1:1 + RW].rearrange("p (h r) -> p h r", h=H)[:, :, 0], final), [m, st["fs"]])

        m_mask = {}

        def weigh(i):
            j, r, u = i // BATCH, i % BATCH + 1, i % sums.RING
            ww = ex[:, j % 2, :, r]
            m_mask[i] = sums.make_masks(i)
            m = act.do(lambda e: e.activation(sums.vals[:, u, D:VALS], ww, ACT.Copy), [ex_ready[j], sums.free(i)])
            for h in range(H):
                hs = slice(h * C, h * C + C)
                m = act.do(lambda e, h=h, hs=hs: e.activation(
                    sums.vals[:, u, hs], vj[:, i % NV, hs], ACT.Copy, scale=ww[:, h:h + 1]), [v_written[i]])
            v_read[i] = ex_read[j] = m

        rest = {}

        def sum_first(p):
            i, j = 2 * p, 2 * p // BATCH
            both = [m[n] for m in (v_read, m_mask) for n in (i + 1, i) if n in m]
            if i % BATCH == 0 and i > 0:
                m = scaled[j] = sums.carry(p, [v_read[i], st["scale", j]], scale=scale[:, j % 2, :])
            else:
                m = sums.carry(p, [v_read[i]])
            rest[p] = [*both, m]
            sums.sum_first(p, both)

        def sum_rest(p):
            sums.sum_rest(p, rest[p])
            sums.keep(p - 1)

        for c in range(NE - 1):
            load_attrs(c)
        todo, begin = {}, 0
        for j in range(batches):
            begin = max(min(T, (j + 1) * BATCH), begin + 8)
            for step in range(8):
                todo.setdefault(begin + step, []).append((j, step))
        AHEAD = NG - 3
        for i in range(AHEAD):
            gather(i)
        edge_product(0)
        for i in range(T + LAG + 4):
            if i < T:
                if i % CH == 0 and i // CH + NE - 1 < -(-T // CH):
                    load_attrs(i // CH + NE - 1)
                if i % BATCH == 0:
                    load_runs(i // BATCH)
                if i % BATCH == RUNS_READY or i == T - 1 and i % BATCH < RUNS_READY:
                    penalties(i // BATCH)
                if i + AHEAD < T:
                    gather(i + AHEAD)
                if i + 1 < T:
                    edge_product(i + 1)
                skip.begin(i, [st.get("ends"), st.get("exc")])
                logits(i)
                st["skip"] = skip.end() or st.get("skip")
            for j, step in todo.get(i, ()):
                setup_step(j, step)
            if 0 <= i - LAG < T:
                weigh(i - LAG)
            n = i - LAG
            if n >= 2 and n % 2 == 0 and n - 2 < T:
                sum_first((n - 2) // 2)
            if n >= 3 and n % 2 == 1 and n - 3 < T:
                sum_rest((n - 3) // 2)
        sums.keep((T - 1) // 2)
        sums.finish()
        skip.finish()



def in_turn(*chains):
    for _ in zip_longest(*chains):
        pass


class NodeTools:

    def __init__(self, ph, n):
        self.ph, self.n = ph, n
        self.stats = ph.sb("stats", [P, n, 6])
        self.mv = ph.sb("mv", [P, n, 2])
        self.rs = ph.sb("rs", [P, n])
        self.eps = ph.sb("eps", [P, 1])
        self.eps_ok = ph.dve.do(lambda e: e.memset(self.eps[:], LN_EPS))
        self.read = {}

    def spread(self, b, x, after, roots):
        dve, act, u = self.ph.dve, self.ph.act, b % self.n
        m = dve.do(lambda e: e.bn_stats(self.stats[:, u, :], x), [*after, self.read.get(b - self.n)])
        yield
        m = dve.do(lambda e: e.bn_aggr(self.mv[:, u, :], self.stats[:, u, :]), [m])
        roots[b] = act.do(lambda e: e.activation(
            self.rs[:, u:u + 1], self.mv[:, u, 1:2], ACT.Sqrt, bias=self.eps[:, 0:1]), [m, self.eps_ok])
        yield

    def normalize(self, b, out, x, after, done):
        dve, u = self.ph.dve, b % self.n
        m = dve.do(lambda e: e.reciprocal(self.rs[:, u:u + 1], self.rs[:, u:u + 1]), after)
        yield
        done[b] = self.read[b] = dve.do(lambda e: e.tensor_scalar(
            out, x, self.mv[:, u, 0:1], self.rs[:, u:u + 1], ALU.subtract, ALU.mult), [m])
        yield


class Turn:

    def __init__(self, ph, k, name):
        self.ph, self.k = ph, k
        self.psum = ph.psum(f"{name}_turn")
        self.cols = ph.sb(f"{name}_cols", [P, 2, KD, P])
        self.copied, self.used, self.kept = {}, {}, {}

    def __call__(self, b, x, after):
        ph, u = self.ph, b % 2
        for a in range(KD):
            m = ph.pe.do(lambda e, a=a: e.transpose(
                self.psum[:, a * P:(a + 1) * P], x[:, a * P:(a + 1) * P], self.k["ident"][:]),
                [*after, self.copied.get(b - 1)])
        self.copied[b] = ph.act.do(lambda e: e.activation(
            self.cols[:, u, :, :].rearrange("p a n -> p (a n)"), self.psum[:, 0:KD * P], ACT.Copy),
            [m, self.used.get(b - 2), self.kept.get(b - 2)])
        return self.copied[b]


class Project:

    PARTS = (0, 2 * D), (2 * D, 3 * D)

    def __init__(self, ph, k, s, t, conv, turn, tables):
        self.ph, self.turn, self.tables = ph, turn, tables
        self.w = ph.sb("w_proj", [P, KD, 3 * D])
        self.bias = ph.sb("b_proj", [P, 3 * D])
        self.psum = [ph.psum("proj0"), ph.psum("proj1")]
        self.rows = ph.sb("proj_rows", [P, 2, 3 * D])
        self.stores, self.col_stores = ph.slots("proj", 2), ph.slots("cols", 2)
        load = ph.slots("proj_w", 1)[0]
        ph.sp.dma(lambda e: e.dma_start(self.w[:], t[f"w_proj{conv}"][:, :, 0:3 * D]), load)
        self.got = ph.sp.dma(lambda e: e.dma_start(self.bias[:], t[f"b_proj{conv}"][:, 0:3 * D].to_broadcast([P, 3 * D])), load)
        self.done, self.added, self.stored = {}, {}, {}

    def products(self, b, cols_ready):
        ph, u = self.ph, b % 2
        """The products; the tensor engine waits for the turned rows, and for the biases of the block
        before to have been added, which frees the psum."""
        cols = self.tables[2]
        self.turn.kept[b] = ph.sp.dma(lambda e: e.dma_start(
            cols[:, :, b * P:(b + 1) * P], self.turn.cols[:, u, :, :]), self.col_stores[u], [cols_ready])
        for half, (lo, hi) in enumerate(self.PARTS):
            for a in range(KD):
                m = ph.pe.do(lambda e, a=a, half=half, lo=lo, hi=hi: e.matmul(
                    self.psum[half][:, 0:hi - lo], self.turn.cols[:, u, a, :], self.w[:, a, lo:hi],
                    start=(a == 0), stop=(a == KD - 1)), [cols_ready, self.got, self.added.get((b - 1, half))])
            self.done[b, half] = self.turn.used[b] = m

    def biased(self, b, half):
        ph, u, (lo, hi) = self.ph, b % 2, self.PARTS[half]
        m = self.added[b, half] = ph.dve.do(lambda e: e.tensor_tensor(
            self.rows[:, u, lo:hi], self.psum[half][:, 0:hi - lo], self.bias[:, lo:hi], ALU.add),
            [self.done[b, half], self.stored.get(b - 2)])
        self.stored[b] = ph.sp.dma(lambda e: e.dma_start(
            self.tables[half][b * P:(b + 1) * P, :], self.rows[:, u, lo:hi]), self.stores[u], [m])

    def finish(self):
        self.ph.sp.hold([(x.sem, x.count) for x in self.stores + self.col_stores])


def gather_sums(ph, k, s, width, table):
    buf = ph.sb("agg", [P, NODE_AHEAD, width])
    slots = ph.slots("agg", NODE_AHEAD)
    marks, read = {}, {}

    def fetch(b):
        if b < s.blocks:
            marks[b] = ph.pool.dma(lambda e: e.indirect_dma_start(
                out=buf[:, b % NODE_AHEAD, :], out_offset=None, **rows_of(table, k["last_row"][:, b:b + 1])),
                slots[b % NODE_AHEAD], [read.get(b - NODE_AHEAD)])

    return buf, marks, read, fetch


def node_pass_resnorm(nc, k, t, s, sums_table, own_table, x1_table, tables):
    with Phase(nc, "n0") as ph:
        pe, dve, act, sp = ph.pe, ph.dve, ph.act, ph.sp
        tools = NodeTools(ph, 2)
        agg, agg_got, agg_read, fetch = gather_sums(ph, k, s, D, sums_table)
        w2 = ph.sb("w2", [P, KD, D])
        x = ph.sb("x", [P, NODE_AHEAD, D])
        own = ph.sb("own", [P, NODE_AHEAD, D])
        y = ph.sb("y", [P, 2, D])
        nb = ph.sb("nb", [P, 2, D])
        o = ph.sb("o", [P, 2, D])
        o2 = ph.sb("o2", [P, 2, D])
        x1 = ph.sb("x1", [P, 3, D])
        ss = ph.sb("ss", [P, 2])
        lin = [ph.psum("lin0"), ph.psum("lin1")]
        turn_y, turn_x = Turn(ph, k, "y"), Turn(ph, k, "x")
        project = Project(ph, k, s, t, 1, turn_x, tables)
        load_w = ph.slots("w", 1)[0]
        m_w = sp.dma(lambda e: e.dma_start(w2[:], t["w2"]), load_w)
        got_x, stores = ph.slots("x", NODE_AHEAD), ph.slots("x1", 3)
        x_mark, x_read, lin_read, lin_done, x1_done, x1_stored, o_read = {}, {}, {}, {}, {}, {}, {}

        def load(b):
            if b < s.blocks:
                u = b % NODE_AHEAD
                sp.dma(lambda e: e.dma_start(x[:, u, :], t["x_rows"][b * P:(b + 1) * P, :]), got_x[u],
                       [x_read.get(b - NODE_AHEAD), lin_read.get(b - NODE_AHEAD)])
                x_mark[b] = sp.dma(lambda e: e.dma_start(own[:, u, :], own_table[b * P:(b + 1) * P, :]), got_x[u])
                fetch(b)

        nb_done, y_done, o_done, roots = {}, {}, {}, {}

        def neighbours(b):
            u = b % 2
            y_done[b] = dve.do(lambda e: e.scalar_tensor_tensor(
                y[:, u, :], x[:, b % NODE_AHEAD, :], 1.0, nb[:, u, :], ALU.add, ALU.mult),
                [nb_done[b], x_mark[b], turn_y.copied.get(b - 2)])

        def neighbour_sum(b):
            u = b % 2
            nb_done[b] = agg_read[b] = act.do(lambda e: e.activation(
                nb[:, u, :], agg[:, b % NODE_AHEAD, :], ACT.Copy, scale=k["has_edge"][:, b:b + 1]), [agg_got[b], y_done.get(b - 2)])

        def linear(b, cols):
            u = b % 2
            for a in range(KD):
                m = pe.do(lambda e, a=a: e.matmul(lin[u][:, 0:D], turn_y.cols[:, u, a, :], w2[:, a, :],
                                                  start=(a == 0), stop=(a == KD - 1)), [cols, m_w, lin_read.get(b - 2)])
            lin_done[b] = turn_y.used[b] = m

        def leaky(b):
            u = b % 2
            m = lin_read[b] = dve.do(lambda e: e.tensor_tensor(o[:, u, :], lin[u][:, 0:D], own[:, b % NODE_AHEAD, :], ALU.add),
                                     [lin_done[b], x_mark[b], o_read.get(b - 2)])
            o_done[b] = dve.do(lambda e: e.scalar_tensor_tensor(
                o2[:, u, :], o[:, u, :], LEAKY, o[:, u, :], ALU.mult, ALU.max), [m])

        def norm(b):
            u = b % 2
            q = act.do(lambda e: e.activation(o[:, u, :], o2[:, u, :], ACT.Square, accum_out=ss[:, u:u + 1]), [o_done[b]])
            roots[b] = act.do(lambda e: e.activation(ss[:, u:u + 1], ss[:, u:u + 1], ACT.Sqrt), [q])

        def residual(b):
            u = b % 2
            q = dve.do(lambda e: e.tensor_scalar(ss[:, u:u + 1], ss[:, u:u + 1], NORM_EPS, None, ALU.max), [roots[b]])
            q = dve.do(lambda e: e.reciprocal(ss[:, u:u + 1], ss[:, u:u + 1]), [q])
            m = x_read[b] = dve.do(lambda e: e.scalar_tensor_tensor(
                o[:, u, :], o2[:, u, :], ss[:, u:u + 1], x[:, b % NODE_AHEAD, :], ALU.mult, ALU.add), [q])
            in_turn(tools.spread(b, o[:, u, :], [m], roots))

        def normalized(b):
            u, v = b % 2, b % 3
            in_turn(tools.normalize(
                b, x1[:, v, :], o[:, u, :], [roots[b], x1_stored.get(b - 3), turn_x.copied.get(b - 3)], x1_done))
            m = o_read[b] = x1_done[b]
            x1_stored[b] = sp.dma(lambda e: e.dma_start(x1_table[b * P:(b + 1) * P, :], x1[:, v, :]), stores[v], [m])

        B = s.blocks
        for b in range(3):
            load(b)
        neighbour_sum(0)
        neighbours(0)
        for b in range(B + 2):
            if b + 1 < B:
                neighbour_sum(b + 1)
            if 0 <= b - 1 < B:
                leaky(b - 1)
            if b >= 2:
                cols_x = turn_x(b - 2, x1[:, (b - 2) % 3, :], [x1_done[b - 2]])
            if b < B:
                cols_y = turn_y(b, y[:, b % 2, :], [y_done[b]])
            if 0 <= b - 1 < B:
                norm(b - 1)
            if b + 1 < B:
                neighbours(b + 1)
            if b >= 2:
                project.products(b - 2, cols_x)
            if b < B:
                linear(b, cols_y)
            if 0 <= b - 1 < B:
                residual(b - 1)
            if b >= 2:
                project.biased(b - 2, 0)
            if 0 <= b - 1 < B:
                normalized(b - 1)
            if b >= 2:
                project.biased(b - 2, 1)
            load(b + 3)
        project.finish()
        sp.hold([(x.sem, x.count) for x in stores])


def conv_rows(ph, k, s, sums_table, skip_table, n):
    agg, agg_got, agg_read, fetch = gather_sums(ph, k, s, VALS, sums_table)
    skip = ph.sb("skip", [P, NODE_AHEAD, D])
    got = ph.slots("skip", NODE_AHEAD)
    rec = ph.sb("rec", [P, n, H])
    rows = ph.sb("rows", [P, n, D])
    marks, read, used = {}, {}, {}

    def load(b):
        if b < s.blocks:
            fetch(b)
            marks[b] = ph.sp.dma(lambda e: e.dma_start(skip[:, b % NODE_AHEAD, :], skip_table[b * P:(b + 1) * P, :]),
                                 got[b % NODE_AHEAD], [read.get(b - NODE_AHEAD)])

    def rows_ready(b):
        dve, u, v = ph.dve, b % n, b % NODE_AHEAD
        m = dve.do(lambda e: e.tensor_scalar(rec[:, u, :], agg[:, v, D:VALS], SUM_EPS, None, ALU.add), [agg_got[b]])
        yield
        m = dve.do(lambda e: e.reciprocal(rec[:, u, :], rec[:, u, :]), [m])
        yield
        m = dve.do(lambda e: e.tensor_scalar(rec[:, u, :], rec[:, u, :], k["has_edge"][:, b:b + 1], None, ALU.mult), [m])
        yield
        m = agg_read[b] = dve.do(lambda e: e.tensor_tensor(
            rows[:, u, :].rearrange("p (h c) -> p h c", h=H), agg[:, v, 0:D].rearrange("p (h c) -> p h c", h=H),
            rec[:, u, :].unsqueeze(2).to_broadcast([P, H, C]), ALU.mult), [m, used.get(b - n)])
        yield
        read[b] = dve.do(lambda e: e.tensor_tensor(rows[:, u, :], rows[:, u, :], skip[:, v, :], ALU.add), [m, marks[b]])
        yield

    return load, rows, rows_ready, read, used


def node_pass_hidden(nc, k, t, s, sums_table, skip_table, tables):
    with Phase(nc, "n1") as ph:
        load, rows, rows_ready, ready, used = conv_rows(ph, k, s, sums_table, skip_table, 2)
        turn = Turn(ph, k, "h")
        project = Project(ph, k, s, t, 2, turn, tables)
        done = {}

        def hidden(b):
            in_turn(rows_ready(b))
            done[b] = ph.dve.do(lambda e: e.tensor_scalar(
                rows[:, b % 2, :], rows[:, b % 2, :], 0.0, None, ALU.max), [ready[b]])

        def turned(b):
            used[b] = turn(b, rows[:, b % 2, :], [done[b]])

        for b in range(NODE_AHEAD):
            load(b)
        for b in range(min(2, s.blocks)):
            hidden(b)
        turned(0)
        for b in range(s.blocks):
            if b + 1 < s.blocks:
                turned(b + 1)
            if b + 2 < s.blocks:
                hidden(b + 2)
            project.products(b, used[b])
            project.biased(b, 0)
            project.biased(b, 1)
            load(b + NODE_AHEAD)
        project.finish()


def node_pass_last(nc, k, t, s, sums_table, skip_table, x1_table, out):
    with Phase(nc, "n2") as ph:
        tools = NodeTools(ph, 4)
        load, rows, rows_ready, ready, used = conv_rows(ph, k, s, sums_table, skip_table, 4)
        x1 = ph.sb("x1", [P, NODE_AHEAD, D])
        y = ph.sb("y", [P, 4, D])
        got, stores = ph.slots("x1", NODE_AHEAD), ph.slots("out", 4)
        marks, read, stored, roots = {}, {}, {}, {}

        def load_all(b):
            load(b)
            if b < s.blocks:
                marks[b] = ph.sp.dma(lambda e: e.dma_start(x1[:, b % NODE_AHEAD, :], x1_table[b * P:(b + 1) * P, :]),
                                     got[b % NODE_AHEAD], [read.get(b - NODE_AHEAD)])

        def residual(b):
            u = b % 4
            yield from rows_ready(b)
            read[b] = ph.dve.do(lambda e: e.tensor_tensor(
                rows[:, u, :], rows[:, u, :], x1[:, b % NODE_AHEAD, :], ALU.add), [ready[b], marks[b]])
            yield
            yield from tools.spread(b, rows[:, u, :], [read[b]], roots)

        def normalized(b):
            return tools.normalize(b, y[:, b % 4, :], rows[:, b % 4, :], [roots[b], stored.get(b - 4)], used)

        for b in range(NODE_AHEAD):
            load_all(b)
        in_turn(*(residual(b) for b in range(min(2, s.blocks))))
        for first in range(0, s.blocks, 2):
            pair = range(first, min(first + 2, s.blocks))
            coming = range(first + 2, min(first + 4, s.blocks))
            in_turn(*(residual(b) for b in coming), *(normalized(b) for b in pair))
            for b in pair:
                n = min(P, s.nodes - b * P)
                stored[b] = ph.sp.dma(lambda e, b=b, n=n: e.dma_start(out[b * P:b * P + n, :], y[0:n, b % 4, :]),
                                      stores[b % 4], [used[b]])
            for b in pair:
                load_all(b + NODE_AHEAD)
        ph.sp.hold([(x.sem, x.count) for x in stores])


def build(nc, t, s, out):
    def scratch(name, shape):
        return nc.dram_tensor(name, shape, F32, kind="Internal").ap()

    slots = s.tiles * P
    sums0, own = scratch("sums0", [slots, D]), scratch("own_rows", [s.rows, D])
    sums = [scratch(f"sums{c}", [slots, VALS]) for c in (1, 2)]
    x1 = scratch("x1_rows", [s.rows, D])
    kv = [scratch(f"kv{c}", [s.rows, 2 * D]) for c in (1, 2)]
    q = [scratch(f"q{c}", [s.rows, D]) for c in (1, 2)]
    cols = [scratch(f"cols{c}", [P, KD, s.rows]) for c in (1, 2)]
    skip = [scratch(f"skip{c}", [s.rows, D]) for c in (1, 2)]
    skip_of = [(cols[c], t[f"w_proj{c + 1}"][:, :, 3 * D:], t[f"b_proj{c + 1}"][:, 3 * D:], skip[c]) for c in (0, 1)]
    with ExitStack() as keep:
        k = constants(nc, keep, t, s)
        edge_pass_weighted(nc, k, t, s, sums0, own)
        node_pass_resnorm(nc, k, t, s, sums0, own, x1, (kv[0], q[0], cols[0]))
        edge_pass_attention(nc, "e1", k, t, s, t["w_edge1"], kv[0], q[0], sums[0], skip_of[0])
        node_pass_hidden(nc, k, t, s, sums[0], skip[0], (kv[1], q[1], cols[1]))
        edge_pass_attention(nc, "e2", k, t, s, t["w_edge2"], kv[1], q[1], sums[1], skip_of[1])
        node_pass_last(nc, k, t, s, sums[1], skip[1], x1, out)



def lay_out(x, src, dst, edge_attr_194, edge_weight, L0_gnn_W1, L0_gnn_b1, L0_gnn_W2, L0_gnn_b2, **conv):
    n, e, f = x.shape[0], src.shape[0], edge_attr_194.shape[1]
    s = Shapes(n, e, f)

    def slots(a, front, behind):
        line = np.full(s.cols, behind, a.dtype)
        line[0], line[1:1 + e] = front, a
        return np.ascontiguousarray(line[np.arange(s.tiles)[:, None] * OWN + np.arange(P)[None, :]])

    def halves(w, rows):
        full = np.zeros((rows * -(-w.shape[0] // rows), w.shape[1]), w.dtype)
        full[:w.shape[0]] = w
        return np.ascontiguousarray(full.reshape(-1, rows, w.shape[1]).transpose(1, 0, 2))

    dst_rows = slots(dst, s.front, s.behind)
    dst_next = dst_rows.copy()
    dst_next[:, 0] = dst_rows[:, 1]
    x_rows = np.zeros((s.rows, x.shape[1]), x.dtype)
    x_rows[:n] = x
    attr = np.zeros((2 * s.ka, s.cols), edge_attr_194.dtype)
    attr[:f, 1:1 + e] = edge_attr_194.T
    t = {
        "dst_rows": dst_rows,
        "dst_cols": np.ascontiguousarray(dst_rows.T),
        "dst_next_cols": np.ascontiguousarray(dst_next.T),
        "src_cols": np.ascontiguousarray(slots(src, 0, 0).T),
        "weight_cols": np.ascontiguousarray(slots(edge_weight, 0, 0).T),
        "x_rows": x_rows,
        "x_cols": halves(x_rows.T, P),
        "attr_cols": np.ascontiguousarray(attr.reshape(2, s.ka, s.cols).transpose(1, 0, 2)),
        "w1": halves(L0_gnn_W1.T, P), "w2": halves(L0_gnn_W2.T, P),
        "b1": L0_gnn_b1[None, :], "b2": L0_gnn_b2[None, :],
    }
    for c in (1, 2):
        g = lambda name: conv[f"L1_gnn_{name}{c}"]
        t[f"w_proj{c}"] = halves(np.concatenate([g("Wk"), g("Wv"), g("Wq"), g("Ws")], axis=1), P)
        t[f"b_proj{c}"] = np.concatenate([g("bk"), g("bv"), g("bq"), g("bs")])[None, :]
        t[f"w_edge{c}"] = halves(g("We"), s.ka)
    return s, {name: np.ascontiguousarray(a) for name, a in t.items()}


def kernel(**inputs):
    import concourse.bacc as _bacc
    from concourse.bass_utils import run_bass_kernel_spmd as _run

    s, arrays = lay_out(**{name: np.asarray(a) for name, a in inputs.items()})
    nc = _bacc.Bacc("TRN2", target_bir_lowering=False, num_devices=1)
    t = {name: nc.dram_tensor(name, a.shape, mybir.dt.from_np(a.dtype), kind="ExternalInput").ap()
         for name, a in arrays.items()}
    out = nc.dram_tensor("out", (s.nodes, D), F32, kind="ExternalOutput").ap()
    build(nc, t, s, out)
    r = _run(nc, [arrays], core_ids=[0])
    return r.results[0]["out"]
```
